# Optimizing a Trainium2 kernel written in Bass

```python
import numpy as np
import jax
import jax.numpy as jnp

def _softmax(x, axis=-1):
    return jax.nn.softmax(x, axis=axis)

def _gelu(x):
    return jax.nn.gelu(x, approximate=True)

def _silu(x):
    return jax.nn.silu(x)

def _sigmoid(x):
    return jax.nn.sigmoid(x)

def _layernorm(x, axis=-1, eps=1e-05):
    m = jnp.mean(x, axis=axis, keepdims=True)
    v = jnp.var(x, axis=axis, keepdims=True)
    return (x - m) / jnp.sqrt(v + eps)

def _scatter_add(tgt, idx, src, axis=0):
    return tgt.at[idx].add(src)

def _segment_sum(src, seg, n):
    return jax.ops.segment_sum(src, seg, n)
kernel_name = 'mk_adj_resnorm_d2_adj_r2_3c1c17'

def setup_inputs(seed: int=0):
    np.random.seed(seed)
    _w = jnp.asarray

    def _rec_inputs():
        import jax
        import jax.numpy as jnp
        _gk = jax.random.key(seed)
        x = 0.0001732 + 1 * jax.random.normal(jax.random.fold_in(_gk, 1), (5120, 64), jnp.float32)
        _a = jax.random.bernoulli(jax.random.fold_in(_gk, 2), 0.000390625, (5120, 5120))
        _af = _a.astype(jnp.float32)
        _af = _af * jax.random.uniform(jax.random.fold_in(_gk, 3), (5120, 5120), jnp.float32, 0.05, 0.02)
        adj = _af
        return (x, adj)
    x, adj = _rec_inputs()

    def _L0_gnn_setup():
        import jax, jax.numpy as jnp
        import numpy as np
        N_USERS = 2048
        N_ITEMS = 3072
        EMB = 64
        LN_EPS = 1e-05
        key = jax.random.key(seed)
        ks = jax.random.split(key, 10)
        N = N_USERS + N_ITEMS
        ego = jax.random.normal(ks[0], (N, EMB), jnp.float32)
        adj = (jax.random.uniform(ks[1], (N, N), jnp.float32) < 0.01).astype(jnp.float32) * 0.02
        xav = float(np.sqrt(6.0 / (EMB + EMB)))
        W_u = jax.random.uniform(ks[2], (EMB, EMB), jnp.float32, -xav, xav)
        W_i = jax.random.uniform(ks[3], (EMB, EMB), jnp.float32, -xav, xav)
        diag_u = jax.random.uniform(ks[4], (N_USERS,), jnp.float32, 0.99, 1.01)
        diag_i = jax.random.uniform(ks[5], (N_ITEMS,), jnp.float32, 0.99, 1.01)
        par_u = jax.random.uniform(ks[6], (2,), jnp.float32, 0.0, 0.99)
        par_i = jax.random.uniform(ks[7], (2,), jnp.float32, 0.0, 0.99)
        ln_gamma = jnp.ones((EMB,), jnp.float32)
        ln_beta = jnp.zeros((EMB,), jnp.float32)
        return {'ego_embeddings': ego, 'adj': adj, 'W_u': W_u, 'diag_u': diag_u, 'par_u': par_u, 'W_i': W_i, 'diag_i': diag_i, 'par_i': par_i, 'ln_gamma': ln_gamma, 'ln_beta': ln_beta}
    _L0_gnn_all = _L0_gnn_setup()
    _L0_gnn_in = {k: v for k, v in _L0_gnn_all.items() if k in ('W_u', 'diag_u', 'par_u', 'W_i', 'diag_i', 'par_i', 'ln_gamma', 'ln_beta')}
    del _L0_gnn_all

    def _L1_gnn_setup():
        import jax, jax.numpy as jnp
        import numpy as np
        N, D, H = (8192, 64, 128)
        GAIN = 0.2
        key = jax.random.key(seed)
        ks = jax.random.split(key, 6)
        X = jax.random.normal(ks[0], (N, D), dtype=jnp.float32)
        t = jax.random.uniform(ks[1], (1,), dtype=jnp.float32)
        Wt = jax.random.uniform(ks[2], (N, N), dtype=jnp.float32)
        B = GAIN * jnp.eye(D, dtype=jnp.float32) + 0.01 * jax.random.normal(ks[3], (D, D), dtype=jnp.float32)
        W1 = jax.random.normal(ks[4], (D + 1, H), dtype=jnp.float32) * (1.0 / np.sqrt(D + 1))
        b1 = jnp.zeros((H,), dtype=jnp.float32)
        W2 = jax.random.normal(ks[5], (H, D), dtype=jnp.float32) * (1.0 / np.sqrt(H))
        b2 = jnp.zeros((D,), dtype=jnp.float32)
        return {'X': X, 't': t, 'Wt': Wt, 'B': B, 'W1': W1, 'b1': b1, 'W2': W2, 'b2': b2}
    _L1_gnn_all = _L1_gnn_setup()
    _L1_gnn_in = {k: v for k, v in _L1_gnn_all.items() if k in ('t', 'B', 'W1', 'b1', 'W2', 'b2')}
    del _L1_gnn_all
    return {'x': x, 'adj': adj, 'L0_gnn_W_u': _L0_gnn_in['W_u'], 'L0_gnn_diag_u': _L0_gnn_in['diag_u'], 'L0_gnn_par_u': _L0_gnn_in['par_u'], 'L0_gnn_W_i': _L0_gnn_in['W_i'], 'L0_gnn_diag_i': _L0_gnn_in['diag_i'], 'L0_gnn_par_i': _L0_gnn_in['par_i'], 'L0_gnn_ln_gamma': _L0_gnn_in['ln_gamma'], 'L0_gnn_ln_beta': _L0_gnn_in['ln_beta'], 'L1_gnn_t': _L1_gnn_in['t'], 'L1_gnn_B': _L1_gnn_in['B'], 'L1_gnn_W1': _L1_gnn_in['W1'], 'L1_gnn_b1': _L1_gnn_in['b1'], 'L1_gnn_W2': _L1_gnn_in['W2'], 'L1_gnn_b2': _L1_gnn_in['b2']}

def reference(x, adj, L0_gnn_W_u, L0_gnn_diag_u, L0_gnn_par_u, L0_gnn_W_i, L0_gnn_diag_i, L0_gnn_par_i, L0_gnn_ln_gamma, L0_gnn_ln_beta, L1_gnn_t, L1_gnn_B, L1_gnn_W1, L1_gnn_b1, L1_gnn_W2, L1_gnn_b2):
    import jax
    import jax.numpy as jnp

    def _L0_gnn_ref(ego_embeddings, adj, W_u, diag_u, par_u, W_i, diag_i, par_i, ln_gamma, ln_beta):
        import jax, jax.numpy as jnp
        import numpy as np
        N_USERS = 2048
        N_ITEMS = 3072
        EMB = 64
        LN_EPS = 1e-05
        nu = diag_u.shape[0]
        res = ego_embeddings
        ego_u = ego_embeddings[:nu]
        ego_i = ego_embeddings[nu:]
        u = par_u[0] * par_u[1] * (diag_u[:, None] * ego_u @ W_u) + ego_u
        i = par_i[0] * par_i[1] * (diag_i[:, None] * ego_i @ W_i) + ego_i
        e = jnp.concatenate([u, i], axis=0)
        h = adj @ (adj.T @ e)
        mu = jnp.mean(h, axis=-1, keepdims=True)
        var = jnp.var(h, axis=-1, keepdims=True)
        out = (h - mu) * jax.lax.rsqrt(var + LN_EPS) * ln_gamma + ln_beta + res
        return out

    def _L1_gnn_ref(X, t, Wt, B, W1, b1, W2, b2):
        import jax, jax.numpy as jnp
        import numpy as np
        N, D, H = (8192, 64, 128)
        GAIN = 0.2
        n = X.shape[0]
        tcol = jnp.broadcast_to(t.reshape(1, 1), (n, 1))
        h = jnp.tanh(jnp.concatenate([X, tcol], axis=1) @ W1 + b1)
        u_intra = h @ W2 + b2
        XB = X @ B.T
        u_comm = Wt @ XB - jnp.sum(Wt, axis=1, keepdims=True) * XB
        return u_intra + u_comm
    x = _layernorm(x + _L0_gnn_ref(x, adj, L0_gnn_W_u, L0_gnn_diag_u, L0_gnn_par_u, L0_gnn_W_i, L0_gnn_diag_i, L0_gnn_par_i, L0_gnn_ln_gamma, L0_gnn_ln_beta), axis=-1)
    x = _layernorm(x + _L1_gnn_ref(x, L1_gnn_t, adj, L1_gnn_B, L1_gnn_W1, L1_gnn_b1, L1_gnn_W2, L1_gnn_b2), axis=-1)
    return x

_drawn_inputs = setup_inputs


def setup_inputs(seed=0):
    import zlib

    import numpy as np

    out = dict(_drawn_inputs(seed))
    spreads = {'L0_gnn_ln_gamma': (1.0, 0.2),
     'L0_gnn_ln_beta': (0.0, 0.1),
     'L1_gnn_b1': (0.0, 0.1),
     'L1_gnn_b2': (0.0, 0.1)}
    factors = {'L0_gnn_diag_u': 8.0, 'L0_gnn_W_i': 6.973, 'L0_gnn_diag_i': 8.0, 'L1_gnn_B': 2.731}
    for name, (base, spread) in spreads.items():
        noise = np.random.default_rng([zlib.crc32(name.encode()), seed]).standard_normal(out[name].shape)
        drawn = base * np.exp(spread * noise) if base else spread * noise
        out[name] = jnp.asarray(drawn.astype(out[name].dtype))
    for name, factor in factors.items():
        out[name] = (out[name] * factor).astype(out[name].dtype)
    return out
```

```python
from contextlib import ExitStack

import concourse.bass as bass
from concourse import mybir

F32 = mybir.dt.float32
BF16 = mybir.dt.bfloat16
ALU = mybir.AluOpType
ACT = mybir.ActivationFunctionType
AX = mybir.AxisListType

P = 128
D = 64
N = 5120
HALVES = 2
CHUNKS = 5
TILES = 4
BANK = TILES * P
ROWS8 = TILES * HALVES
HIDDEN = 128
N_USERS = 2048
USER_CHUNKS = N_USERS // BANK
PANELS = CHUNKS * TILES
SLOTS = TILES
GROUPS = CHUNKS * TILES
PIECE = HALVES * HALVES * BANK
PANEL = CHUNKS * PIECE
STAGES = 2
EPS = 1e-5

CHUNK_ORDER = [CHUNKS - 1] + list(range(CHUNKS - 1))
SECOND_AFTER = [2, 4, 6, 8, 10, 12, 14, 16]


def gnn_kernel(nc, adj, x, diag, par, w_u, w_i, gamma, beta, tval, b_t, w1, b1, w2, b2, out):
    with ExitStack() as ctx:
        def sb(name, shape, dt=F32):
            return ctx.enter_context(nc.sbuf_tensor(name, shape, dt))

        def sem(name):
            return ctx.enter_context(nc.semaphore(name))

        ring = sb("ring", [P, SLOTS * PANEL])
        xrow = sb("xrow", [P, CHUNKS * BANK])
        e_ht = sb("e_ht", [P, CHUNKS * BANK])
        nat_xb = sb("nat_xb", [P, CHUNKS * BANK])
        sums_part = sb("sums_part", [P, PANELS * GROUPS * HALVES])
        rowsum = sb("rowsum", [P, GROUPS * HALVES])
        ident = sb("ident", [P, P])
        stacked = sb("stacked", [P, D])
        w_ui = sb("w_ui", [P, P])
        w_ii = sb("w_ii", [P, P])
        bb = sb("bb", [P, P])
        w1_sb = sb("w1_sb", [P, HIDDEN])
        w2_sb = sb("w2_sb", [HIDDEN, D])
        gamma_sb = sb("gamma_sb", [P, D])
        beta_sb = sb("beta_sb", [P, D])
        par_sb = sb("par_sb", [P, 4])
        par_prod = sb("par_prod", [P, 2])
        diag_sb = sb("diag_sb", [P, GROUPS * HALVES])
        scale = sb("scale", [P, GROUPS * HALVES])
        t_sb = sb("t_sb", [P, 1])
        w1_t = sb("w1_t", [P, 1])
        b1_sb = sb("b1_sb", [P, 1])
        b1_t = sb("b1_t", [P, 1])
        b2_sb = sb("b2_sb", [P, 1])
        eps_sb = sb("eps_sb", [P, 1])
        zeros = sb("zeros", [P, BANK], BF16)
        yt_sb = sb("yt_sb", [P, HALVES * P])
        y_sb = sb("y_sb", [P, HALVES * D])
        work = sb("work", [P, BANK])
        th = sb("th", [P, BANK])
        xb_stage = sb("xb_stage", [P, SLOTS * HALVES * D])
        stats = sb("stats", [P, ROWS8 * 6])
        moments = sb("moments", [P, ROWS8 * 2])
        deviation = sb("deviation", [P, ROWS8])
        inverse = sb("inverse", [P, ROWS8])

        acc = ctx.enter_context(nc.psum_tensor("acc", [P, CHUNKS, BANK], F32))
        bank_a = ctx.enter_context(nc.psum_tensor("bank_a", [P, BANK], F32))
        bank_v = ctx.enter_context(nc.psum_tensor("bank_v", [P, BANK], F32))
        bank_y = ctx.enter_context(nc.psum_tensor("bank_y", [P, BANK], F32))

        def piece(slot, c, f, h):
            at = slot * PANEL + c * PIECE + (f * HALVES + h) * BANK
            return ring[:, at:at + BANK]

        xt = ring[:, 3 * PANEL:3 * PANEL + CHUNKS * BANK]

        def chunk(tile, c):
            return tile[:, c * BANK:(c + 1) * BANK]

        def rows(ap):
            return ap.rearrange("p (k d) -> p k d", d=D)

        def e_tile(c, t, h):
            at = c * BANK + (t * HALVES + h) * D
            return e_ht[:, at:at + D]

        def turned(g, h):
            at = ((g % STAGES) * HALVES + h) * HALVES * P
            return nat_xb[:, at:at + HALVES * P]

        def turn_bank(g, h):
            return (bank_v if g % 2 else bank_a)[:, h * HALVES * P:(h + 1) * HALVES * P]

        def tanh_part(n):
            return (work if n % 2 else th)[:, :]

        yt_ps = bank_y[:, 0:HALVES * P]
        y_ps = bank_y[:, HALVES * P:HALVES * P + HALVES * D]

        x_loaded = sem("x_loaded")
        small_loaded = sem("small_loaded")
        landed = [[sem(f"landed_{s}_{c}") for c in range(CHUNKS)] for s in range(SLOTS)]
        cleared = sem("cleared")
        ident_ready = sem("ident_ready")
        zeros_ready = sem("zeros_ready")
        scale_step = sem("scale_step")
        x_turned = sem("x_turned")
        xt_copied = sem("xt_copied")
        xw_ready = sem("xw_ready")
        xw_scaled = sem("xw_scaled")
        e_ready = sem("e_ready")
        x2_step = sem("x2_step")
        act_turned = sem("act_turned")
        dve_turned = sem("dve_turned")
        act_copied = sem("act_copied")
        dve_copied = sem("dve_copied")
        first_done = sem("first_done")
        yt_copied = sem("yt_copied")
        y_summed = sem("y_summed")
        y_copied = sem("y_copied")
        second_done = sem("second_done")
        rowsum_ready = sem("rowsum_ready")
        ht_copied = sem("ht_copied")
        h_turned = sem("h_turned")
        stats_ready = sem("stats_ready")
        moments_ready = sem("moments_ready")
        deviation_ready = sem("deviation_ready")
        inverse_ready = sem("inverse_ready")
        normed = sem("normed")
        gamma_step = sem("gamma_step")
        x1_turned = sem("x1_turned")
        x1t_copied = sem("x1t_copied")
        xb_ready = sem("xb_ready")
        xb_copied = sem("xb_copied")
        xb_staged = sem("xb_staged")
        third_done = sem("third_done")
        hidden_ready = sem("hidden_ready")
        tanh_ready = sem("tanh_ready")
        mlp_done = sem("mlp_done")
        scaled_xb = sem("scaled_xb")
        base_ready = sem("base_ready")
        ut_copied = sem("ut_copied")
        u_turned = sem("u_turned")
        z_ready = sem("z_ready")
        stored = sem("stored")

        SMALL = [
            (w_ui[0:D, 0:D], w_u), (w_ui[D:P, D:P], w_i), (w_ii[0:D, 0:D], w_i), (w_ii[D:P, D:P], w_i),
            (par_sb[:, :], par.partition_broadcast(P)), (diag_sb[:, :], diag),
            (bb[0:D, 0:D], b_t), (bb[D:P, D:P], b_t),
            (w1_sb[0:D, :], w1[0:D, :]), (w1_sb[D:P, :], w1[0:D, :]), (w2_sb[:, :], w2),
            (gamma_sb[:, :], gamma.partition_broadcast(P)), (beta_sb[:, :], beta.partition_broadcast(P)),
            (t_sb[:, :], tval.partition_broadcast(P)),
            (w1_t[:, :], w1[D:D + 1, :].rearrange("a n -> n a")), (b1_sb[:, :], b1),
            (b2_sb[0:D, :], b2), (b2_sb[D:P, :], b2),
        ]
        SMALL_ALL = 16 * len(SMALL)

        block = ctx.enter_context(nc.Block())

        @block.sync
        def _(sp):
            sp.dma_start(xrow[:, :], x).then_inc(x_loaded, 16)

            def load(panel, slot, c):
                at = slot * PANEL + c * PIECE
                sp.dma_start(ring[:, at:at + PIECE], adj[bass.ds((panel * CHUNKS + c) * P, P), :]
                             ).then_inc(landed[slot][c], 16)

            for slot in range(SLOTS):
                if slot == 3:
                    sp.wait_ge(xw_ready, CHUNKS)
                for c in range(CHUNKS):
                    load(slot, slot, c)
            with sp.Fori(1, CHUNKS) as k:
                for slot in range(SLOTS):
                    sp.wait_ge(second_done, k * (SLOTS * CHUNKS) + (slot + 1 - SLOTS) * CHUNKS)
                    for c in range(CHUNKS):
                        load(k * SLOTS + slot, slot, c)
            with sp.Fori(0, CHUNKS - 1) as k:
                for slot in range(SLOTS):
                    sp.wait_ge(third_done, k * (SLOTS * CHUNKS) + (slot + 1) * CHUNKS)
                    for c in range(CHUNKS):
                        load(k * SLOTS + slot, slot, c)
            for c in range(CHUNKS):
                sp.wait_ge(normed, 2 * CHUNKS + c + 1)
                sp.dma_start(out[:, c * BANK:(c + 1) * BANK], chunk(xrow, c)).then_inc(stored, 16)
            sp.wait_ge(stored, 16 * CHUNKS)

        @block.gpsimd
        def _(pool):
            nc.gpsimd.memset(w_ui[:, :], 0.0)
            nc.gpsimd.memset(w_ii[:, :], 0.0)
            nc.gpsimd.memset(bb[:, :], 0.0).then_inc(cleared, 1)
            nc.gpsimd.memset(ident[:, :], 0.0).then_inc(ident_ready, 1)
            pool.wait_ge(ident_ready, 1)
            nc.gpsimd.affine_select(out=ident[:, :], in_=ident[:, :], compare_op=ALU.not_equal, fill=1.0,
                                    base=0, pattern=[[-1, P]], channel_multiplier=1).then_inc(ident_ready, 1)
            pool.wait_ge(ident_ready, 2)
            nc.gpsimd.tensor_tensor(stacked[:, :], ident[:, 0:D], ident[:, D:P], ALU.add).then_inc(ident_ready, 1)
            pool.wait_ge(e_ready, CHUNKS)
            pool.wait_ge(small_loaded, SMALL_ALL)
            nc.gpsimd.tensor_tensor(xrow[:, :], xrow[:, :], xrow[:, :], ALU.add).then_inc(x2_step, 1)
            pool.wait_ge(x2_step, 1)
            tiles = GROUPS * HALVES
            nc.gpsimd.tensor_tensor(rows(xrow[:, :]), rows(xrow[:, :]),
                                    beta_sb[:, :].unsqueeze(1).to_broadcast([P, tiles, D]),
                                    ALU.add).then_inc(x2_step, 1)
            pool.wait_ge(x2_step, 2)
            for q, c in enumerate(CHUNK_ORDER):
                pool.wait_ge(normed, 2 * q + 1)
                nc.gpsimd.tensor_tensor(rows(work[:, :]), rows(work[:, :]),
                                        gamma_sb[:, :].unsqueeze(1).to_broadcast([P, ROWS8, D]),
                                        ALU.mult).then_inc(gamma_step, 1)
                pool.wait_ge(gamma_step, 2 * q + 1)
                nc.gpsimd.tensor_tensor(work[:, :], work[:, :], chunk(xrow, c), ALU.add).then_inc(gamma_step, 1)
            with pool.Fori(0, CHUNKS - 1) as k:
                for slot in range(SLOTS):
                    pool.wait_ge(third_done, k * (SLOTS * CHUNKS) + (slot + 1) * CHUNKS)
                    pool.wait_ge(xb_copied, k + 2)
                    nc.gpsimd.tensor_copy(
                        xb_stage[:, slot * HALVES * D:(slot + 1) * HALVES * D],
                        nat_xb[:, bass.ds(k * BANK + slot * HALVES * D, HALVES * D)]).then_inc(xb_staged, 1)
            pool.wait_ge(rowsum_ready, 1)
            pool.wait_ge(x1_turned, CHUNKS)
            pool.wait_ge(xb_staged, SLOTS * (CHUNKS - 1))
            for c in range(CHUNKS):
                nc.gpsimd.tensor_tensor(
                    rows(chunk(nat_xb, c)), rows(chunk(nat_xb, c)),
                    rowsum[:, c * ROWS8:(c + 1) * ROWS8].unsqueeze(2).to_broadcast([P, ROWS8, D]),
                    ALU.mult).then_inc(scaled_xb, 1)
                pool.wait_ge(scaled_xb, c + 1)
                nc.gpsimd.tensor_tensor(chunk(xrow, c), chunk(xrow, c), chunk(nat_xb, c),
                                        ALU.subtract).then_inc(base_ready, 1)

        @block.scalar
        def _(act):
            act.wait_ge(cleared, 1)
            for dst, src in SMALL:
                act.dma_start(dst, src).then_inc(small_loaded, 16)
            for c in range(CHUNKS):
                act.wait_ge(x_turned, c + 1)
                nc.scalar.copy(chunk(xt, c), acc[:, c, :]).then_inc(xt_copied, 1)
            with act.Fori(0, PANELS) as n:
                for g in range(0, GROUPS, 2):
                    act.wait_ge(act_turned, n * (GROUPS // 2) + (g // 2 + 1))
                    for h in range(HALVES):
                        last = nc.scalar.activation(
                            turned(g, h), turn_bank(g, h), ACT.Copy,
                            accum_out=sums_part[:, bass.ds(n * (GROUPS * HALVES) + (g * HALVES + h), 1)])
                    last.then_inc(act_copied, 1)
            for q, c in enumerate(CHUNK_ORDER):
                act.wait_ge(second_done, (PANELS - 1) * CHUNKS + q + 1)
                nc.scalar.copy(chunk(e_ht, c), acc[:, c, :]).then_inc(ht_copied, 1)
            for q, c in enumerate(CHUNK_ORDER):
                for layer in range(2):
                    act.wait_ge(moments_ready, 2 * q + layer + 1)
                    nc.scalar.activation(deviation[:, :], moments[:, 1:2 * ROWS8:2], ACT.Sqrt,
                                         bias=eps_sb[:, 0:1]).then_inc(deviation_ready, 1)
                act.wait_ge(x1_turned, q + 1)
                nc.scalar.copy(chunk(e_ht, c), bank_v[:, :]).then_inc(x1t_copied, 1)
                act.wait_ge(xb_ready, q + 1)
                nc.scalar.copy(chunk(nat_xb, c), bank_y[:, :]).then_inc(xb_copied, 1)
            for n in range(CHUNKS * HALVES):
                act.wait_ge(hidden_ready, n + 1)
                if n >= 2:
                    act.wait_ge(mlp_done, n - 1)
                nc.scalar.activation(tanh_part(n),
                                     (bank_y if n % 2 else bank_v)[:, :], ACT.Tanh,
                                     bias=b1_t[:, 0:1]).then_inc(tanh_ready, 1)
            for c in range(CHUNKS):
                act.wait_ge(third_done, (PANELS - 1) * CHUNKS + c + 1)
                nc.scalar.activation(chunk(e_ht, c), acc[:, c, :], ACT.Identity,
                                     bias=b2_sb[:, 0:1]).then_inc(ut_copied, 1)
                if c > 0:
                    act.wait_ge(moments_ready, 2 * CHUNKS + c)
                    nc.scalar.activation(deviation[:, :], moments[:, 1:2 * ROWS8:2], ACT.Sqrt,
                                         bias=eps_sb[:, 0:1]).then_inc(deviation_ready, 1)
            act.wait_ge(moments_ready, 3 * CHUNKS)
            nc.scalar.activation(deviation[:, :], moments[:, 1:2 * ROWS8:2], ACT.Sqrt,
                                 bias=eps_sb[:, 0:1]).then_inc(deviation_ready, 1)

        @block.vector
        def _(dve):
            nc.vector.memset(zeros[:, :], 0.0)
            nc.vector.memset(eps_sb[:, :], EPS).then_inc(zeros_ready, 1)
            dve.wait_ge(small_loaded, SMALL_ALL)
            nc.vector.tensor_tensor(par_prod[:, 0:2], par_sb[:, 0:4:2], par_sb[:, 1:4:2],
                                    ALU.mult).then_inc(scale_step, 1)
            dve.wait_ge(scale_step, 1)
            nc.vector.tensor_scalar(scale[:, :], diag_sb[:, :], par_prod[:, 1:2], None,
                                    ALU.mult).then_inc(scale_step, 1)
            dve.wait_ge(scale_step, 2)
            users = USER_CHUNKS * ROWS8
            nc.vector.tensor_scalar(scale[:, 0:users:HALVES], diag_sb[:, 0:users:HALVES], par_prod[:, 0:1], None,
                                    ALU.mult).then_inc(scale_step, 1)
            nc.vector.scalar_tensor_tensor(out=b1_t[:, :], in0=w1_t[:, :], scalar=t_sb[:, 0:1], in1=b1_sb[:, :],
                                           op0=ALU.mult, op1=ALU.add).then_inc(scale_step, 1)
            dve.wait_ge(scale_step, 4)
            dve.wait_ge(x_loaded, 16)
            for c in range(CHUNKS):
                dve.wait_ge(xw_ready, c + 1)
                nc.vector.tensor_tensor(
                    rows(chunk(e_ht, c)), rows(acc[:, c, :]),
                    scale[:, c * ROWS8:(c + 1) * ROWS8].unsqueeze(2).to_broadcast([P, ROWS8, D]),
                    ALU.mult).then_inc(xw_scaled, 1)
                dve.wait_ge(xw_scaled, c + 1)
                nc.vector.tensor_tensor(chunk(e_ht, c), chunk(e_ht, c), chunk(xrow, c),
                                        ALU.add).then_inc(e_ready, 1)
            with dve.Fori(0, PANELS) as n:
                for g in range(1, GROUPS, 2):
                    dve.wait_ge(dve_turned, n * (GROUPS // 2) + (g // 2 + 1))
                    for h in range(HALVES):
                        last = nc.vector.tensor_scalar(
                            turned(g, h), turn_bank(g, h), 1.0, None, ALU.mult, ALU.add,
                            accum_out=sums_part[:, bass.ds(n * (GROUPS * HALVES) + (g * HALVES + h), 1)])
                    last.then_inc(dve_copied, 1)
                dve.wait_ge(first_done, n + 1)
                nc.vector.tensor_copy(yt_sb[:, :], yt_ps).then_inc(yt_copied, 1)
                dve.wait_ge(y_summed, n + 1)
                nc.vector.tensor_copy(y_sb[:, :], y_ps).then_inc(y_copied, 1)

            def inverse_deviations(src, n):
                for k in range(ROWS8):
                    last = nc.vector.bn_stats(stats[:, k * 6:(k + 1) * 6], src[:, k * D:(k + 1) * D])
                last.then_inc(stats_ready, 1)
                dve.wait_ge(stats_ready, n + 1)
                for k in range(ROWS8):
                    last = nc.vector.bn_aggr(moments[:, k * 2:(k + 1) * 2], stats[:, k * 6:(k + 1) * 6])
                last.then_inc(moments_ready, 1)
                dve.wait_ge(deviation_ready, n + 1)
                nc.vector.reciprocal(inverse[:, :], deviation[:, :]).then_inc(inverse_ready, 1)
                dve.wait_ge(inverse_ready, n + 1)

            def normalise(dst, src):
                for k in range(ROWS8):
                    last = nc.vector.tensor_scalar(dst[:, k * D:(k + 1) * D], src[:, k * D:(k + 1) * D],
                                                   moments[:, 2 * k:2 * k + 1], inverse[:, k:k + 1],
                                                   ALU.subtract, ALU.mult)
                last.then_inc(normed, 1)

            dve.wait_ge(x2_step, 2)
            for q, c in enumerate(CHUNK_ORDER):
                dve.wait_ge(h_turned, q + 1)
                inverse_deviations(bank_a, 2 * q)
                normalise(work, bank_a)
                dve.wait_ge(gamma_step, 2 * q + 2)
                inverse_deviations(work, 2 * q + 1)
                normalise(chunk(xrow, c), work)
                dve.wait_ge(normed, 2 * q + 2)
                if q == 0:
                    dve.wait_ge(act_copied, PANELS * GROUPS // 2)
                    nc.vector.tensor_reduce(
                        rowsum[:, :], sums_part[:, :].rearrange("p (n k) -> p k n", n=PANELS),
                        AX.X, ALU.add).then_inc(rowsum_ready, 1)
            for c in range(CHUNKS):
                dve.wait_ge(u_turned, c + 1)
                dve.wait_ge(base_ready, c + 1)
                nc.vector.tensor_tensor(chunk(xrow, c), (bank_a, bank_v, bank_y)[c % 3][:, :], chunk(xrow, c),
                                        ALU.add).then_inc(z_ready, 1)
                dve.wait_ge(z_ready, c + 1)
                inverse_deviations(chunk(xrow, c), 2 * CHUNKS + c)
                normalise(chunk(xrow, c), chunk(xrow, c))
                dve.wait_ge(normed, 2 * CHUNKS + c + 1)

        @block.tensor
        def _(pe):
            def turn_chunk(bank, tile, c, done):
                for t in range(TILES):
                    at = c * BANK + t * P
                    last = pe.transpose(bank[:, t * P:(t + 1) * P], tile[:, at:at + P], ident[:, :])
                last.then_inc(done, 1)

            def times_blocks(bank, tile_t, c, blocks, done):
                for t in range(TILES):
                    at = c * BANK + t * P
                    last = pe.matmul(bank[:, t * P:(t + 1) * P], tile_t[:, at:at + P], blocks[:, :],
                                     start=True, stop=True)
                last.then_inc(done, 1)

            pe.wait_ge(x_loaded, 16)
            pe.wait_ge(ident_ready, 3)
            pe.wait_ge(small_loaded, SMALL_ALL)
            pe.wait_ge(zeros_ready, 1)
            for c in range(CHUNKS):
                turn_chunk(acc[:, c, :], xrow, c, x_turned)
            for c in range(CHUNKS):
                pe.wait_ge(xt_copied, c + 1)
                times_blocks(acc[:, c, :], xt, c, w_ui if c < USER_CHUNKS else w_ii, xw_ready)
            for c in range(CHUNKS):
                pe.wait_ge(xw_scaled, c + 1)
                last = pe.matmul(acc[:, c, :], zeros[:, 0:P], zeros[:, :], start=True, stop=False,
                                 skip_group_check=True)
            pe.wait_ge(e_ready, CHUNKS)

            def copied_by(g):
                return dve_copied if g % 2 else act_copied

            def turn_group(k, u, g):
                c, t = divmod(g, TILES)
                if t == 0:
                    pe.wait_ge(landed[u][c], k * 16 + 16)
                for h in range(HALVES):
                    for f in range(HALVES):
                        last = pe.transpose(turn_bank(g, h)[:, f * P:(f + 1) * P],
                                            piece(u, c, f, h)[:, t * P:(t + 1) * P], ident[:, :])
                last.then_inc(dve_turned if g % 2 else act_turned, 1)

            def first_product(k, u, g):
                c, t = divmod(g, TILES)
                pe.wait_ge(copied_by(g), k * (SLOTS * GROUPS // 2) + ((u * GROUPS + g) // 2 + 1))
                for h in range(HALVES):
                    last = pe.matmul(yt_ps[h * D:(h + 1) * D, :], e_tile(c, t, h), turned(g, h),
                                     start=(g == 0), stop=(g == GROUPS - 1))
                if g == GROUPS - 1:
                    last.then_inc(first_done, 1)

            def second_product(k, u, part):
                c, f = CHUNK_ORDER[part // HALVES], part % HALVES
                if part == 0:
                    pe.wait_ge(y_copied, k * SLOTS + (u + 1))
                for h in range(HALVES):
                    last = pe.matmul(acc[h * D:(h + 1) * D, c, :], y_sb[:, f * D:(f + 1) * D], piece(u, c, f, h),
                                     start=False, stop=False, skip_group_check=True)
                if f == HALVES - 1:
                    last.then_inc(second_done, 1)

            def sum_y(k, u):
                pe.wait_ge(yt_copied, k * SLOTS + (u + 1))
                for f in range(HALVES):
                    last = pe.matmul(y_ps[:, f * D:(f + 1) * D], yt_sb[:, f * P:(f + 1) * P], stacked[:, :],
                                     start=True, stop=True)
                last.then_inc(y_summed, 1)

            with pe.Fori(0, CHUNKS) as k:
                for u in range(SLOTS):
                    turn_group(k, u, 0)
                    turn_group(k, u, 1)
                    if u > 0:
                        second_product(k, u - 1, 0)
                    part = 1
                    for g in range(GROUPS):
                        first_product(k, u, g)
                        if g + 2 < GROUPS:
                            turn_group(k, u, g + 2)
                        if u > 0 and g in SECOND_AFTER[:-1]:
                            second_product(k, u - 1, part)
                            part += 1
                    while u > 0 and part < CHUNKS * HALVES:
                        second_product(k, u - 1, part)
                        part += 1
                    sum_y(k, u)
                for part in range(CHUNKS * HALVES):
                    second_product(k, SLOTS - 1, part)

            def third_product(u, weights, first):
                for c in range(CHUNKS):
                    for f in range(HALVES):
                        for h in range(HALVES):
                            last = pe.matmul(acc[h * D:(h + 1) * D, c, :], weights[:, f * D:(f + 1) * D],
                                             piece(u, c, f, h), start=(first and f == 0), stop=False,
                                             skip_group_check=True)
                    last.then_inc(third_done, 1)

            pe.wait_ge(ht_copied, 1)
            turn_chunk(bank_a, e_ht, CHUNK_ORDER[0], h_turned)
            for q, c in enumerate(CHUNK_ORDER):
                if q > 0:
                    if q == 1:
                        pe.wait_ge(ht_copied, CHUNKS)
                        pe.wait_ge(xb_copied, 1)
                    third_product(q - 1, nat_xb[:, (CHUNKS - 1) * BANK + (q - 1) * HALVES * D:
                                                (CHUNKS - 1) * BANK + q * HALVES * D], q == 1)
                pe.wait_ge(normed, 2 * q + 2)
                if q > 0:
                    pe.wait_ge(x1t_copied, q)
                turn_chunk(bank_v, xrow, c, x1_turned)
                if q + 1 < CHUNKS:
                    pe.wait_ge(ht_copied, q + 2)
                    turn_chunk(bank_a, e_ht, CHUNK_ORDER[q + 1], h_turned)
                pe.wait_ge(x1t_copied, q + 1)
                if q > 0:
                    pe.wait_ge(xb_copied, q)
                times_blocks(bank_y, e_ht, c, bb, xb_ready)

            def hidden(n):
                c, h = divmod(n, HALVES)
                if n >= 2:
                    pe.wait_ge(tanh_ready, n - 1)
                elif n == 1:
                    pe.wait_ge(xb_copied, CHUNKS)
                pe.matmul((bank_y if n % 2 else bank_v)[:, :], w1_sb[h * D:(h + 1) * D, :],
                          e_ht[h * D:(h + 1) * D, c * BANK:(c + 1) * BANK],
                          start=True, stop=True).then_inc(hidden_ready, 1)

            hidden(0)
            for n in range(CHUNKS * HALVES):
                c, h = divmod(n, HALVES)
                if n + 1 < CHUNKS * HALVES:
                    hidden(n + 1)
                pe.wait_ge(tanh_ready, n + 1)
                pe.matmul(acc[h * D:(h + 1) * D, c, :], w2_sb[:, :], tanh_part(n),
                          start=False, stop=False, skip_group_check=True).then_inc(mlp_done, 1)

            with pe.Fori(0, CHUNKS - 1) as k:
                for u in range(SLOTS):
                    pe.wait_ge(xb_staged, k * SLOTS + (u + 1))
                    for c in range(CHUNKS):
                        pe.wait_ge(landed[u][c], k * 16 + 16 * (CHUNKS + 1))
                    third_product(u, xb_stage[:, u * HALVES * D:(u + 1) * HALVES * D], False)

            for c in range(CHUNKS):
                pe.wait_ge(ut_copied, c + 1)
                if c >= 3:
                    pe.wait_ge(z_ready, c - 2)
                turn_chunk((bank_a, bank_v, bank_y)[c % 3], e_ht, c, u_turned)


def kernel(x, adj, L0_gnn_W_u, L0_gnn_diag_u, L0_gnn_par_u, L0_gnn_W_i, L0_gnn_diag_i, L0_gnn_par_i,
           L0_gnn_ln_gamma, L0_gnn_ln_beta, L1_gnn_t, L1_gnn_B, L1_gnn_W1, L1_gnn_b1, L1_gnn_W2, L1_gnn_b2):
    import numpy as np
    import concourse.bacc as bacc
    from concourse.bass_utils import run_bass_kernel_spmd

    nc = bacc.Bacc("TRN2", target_bir_lowering=False, num_devices=1)
    a6 = np.asarray(adj).reshape(HALVES, CHUNKS, BANK, HALVES, CHUNKS, TILES, P)
    laid = {
        "adj": a6.transpose(4, 5, 1, 6, 3, 0, 2).reshape(PANELS * CHUNKS * P, PIECE),
        "x": np.asarray(x).reshape(HALVES, CHUNKS, TILES, P, D).transpose(3, 1, 2, 0, 4).reshape(P, CHUNKS * BANK),
        "diag": np.concatenate([L0_gnn_diag_u, L0_gnn_diag_i]).reshape(HALVES, CHUNKS, TILES, P)
        .transpose(3, 1, 2, 0).reshape(P, GROUPS * HALVES),
        "par": np.concatenate([L0_gnn_par_u, L0_gnn_par_i]),
        "w_u": L0_gnn_W_u, "w_i": L0_gnn_W_i, "gamma": L0_gnn_ln_gamma, "beta": L0_gnn_ln_beta,
        "tval": L1_gnn_t, "b_t": np.asarray(L1_gnn_B).T, "w1": L1_gnn_W1,
        "b1": np.asarray(L1_gnn_b1).reshape(HIDDEN, 1), "w2": L1_gnn_W2,
        "b2": np.asarray(L1_gnn_b2).reshape(D, 1),
    }
    arrays, args = {}, {}
    for name, a in laid.items():
        a = np.ascontiguousarray(a)
        arrays["in_" + name] = a
        args[name] = nc.dram_tensor("in_" + name, a.shape, mybir.dt.from_np(a.dtype), kind="ExternalInput").ap()
    args["out"] = nc.dram_tensor("out_rows", (P, CHUNKS * BANK), F32, kind="ExternalOutput").ap()
    gnn_kernel(nc, **args)
    r = run_bass_kernel_spmd(nc, [arrays], core_ids=[0])
    got = r.results[0]["out_rows"].reshape(P, CHUNKS, TILES, HALVES, D).transpose(3, 1, 2, 0, 4)
    return np.ascontiguousarray(got.reshape(N, D))
```

```python
from contextlib import ExitStack

import concourse.bass as bass
from concourse import mybir

F32 = mybir.dt.float32
BF16 = mybir.dt.bfloat16
ALU = mybir.AluOpType
ACT = mybir.ActivationFunctionType
AX = mybir.AxisListType

P = 128
D = 64
N = 5120
HALVES = 2
CHUNKS = 5
TILES = 4
BANK = TILES * P
ROWS8 = TILES * HALVES
HIDDEN = 128
N_USERS = 2048
USER_CHUNKS = N_USERS // BANK
PANELS = CHUNKS * TILES
SLOTS = TILES
GROUPS = CHUNKS * TILES
PIECE = HALVES * HALVES * BANK
PANEL = CHUNKS * PIECE
STAGES = 2
GROUP = HALVES * HALVES * P
TURNED = [(c, t) for c in (0, 2, 4) for t in range(TILES)]
LOADED = [(c, t) for c in (1, 3) for t in range(TILES)]
PAIRS = len(LOADED) // 2
SEGMENTS = len(TURNED) // 2
EPS = 1e-5

CHUNK_ORDER = [CHUNKS - 1] + list(range(CHUNKS - 1))
LOADED_IN = [1, 1, 2, 1, 1, 2]
SECOND_IN = [1, 1, 2, 1, 1, 2]
SUMS_IN = [0, 2, 3, 4]


def gnn_kernel(nc, adj, adj_rows, x, matrices, columns, lines, out):
    with ExitStack() as ctx:
        def sb(name, shape, dt=F32):
            return ctx.enter_context(nc.sbuf_tensor(name, shape, dt))

        def sem(name):
            return ctx.enter_context(nc.semaphore(name))

        ring = sb("ring", [P, SLOTS * PANEL])
        xrow = sb("xrow", [P, CHUNKS * BANK])
        e_ht = sb("e_ht", [P, CHUNKS * BANK])
        scratch = sb("scratch", [P, PAIRS * 2 * GROUP + STAGES * GROUP])
        sums_part = sb("sums_part", [P, PANELS * GROUPS * HALVES])
        rowsum = sb("rowsum", [P, GROUPS * HALVES])
        ident = sb("ident", [P, P])
        stacked = sb("stacked", [P, D])
        columns_sb = sb("columns_sb", [P, columns.shape[1]])
        lines_sb = sb("lines_sb", [P, lines.shape[0]])
        par_prod = sb("par_prod", [P, 2])
        scale = sb("scale", [P, GROUPS * HALVES])
        b1_t = sb("b1_t", [P, 1])
        eps_sb = sb("eps_sb", [P, 1])
        table_warm = sb("table_warm", [P, 2])
        yt_sb = sb("yt_sb", [P, HALVES * P])
        y_sb = sb("y_sb", [P, HALVES * D])

        acc = ctx.enter_context(nc.psum_tensor("acc", [P, CHUNKS, BANK], F32))
        bank_a = ctx.enter_context(nc.psum_tensor("bank_a", [P, BANK], F32))
        bank_v = ctx.enter_context(nc.psum_tensor("bank_v", [P, BANK], F32))
        bank_y = ctx.enter_context(nc.psum_tensor("bank_y", [P, BANK], F32))

        def piece(slot, c, f, h):
            at = slot * PANEL + c * PIECE + (f * HALVES + h) * BANK
            return ring[:, at:at + BANK]

        stage_at = PAIRS * 2 * GROUP
        matrices_sb = scratch[:, stage_at:stage_at + 2 * P]
        w_ui = matrices_sb[:, 0:P]
        w_ii = matrices_sb[:, P:2 * P]
        widths = [P, HIDDEN, D, GROUPS * HALVES, 1, 1, 1]
        ends = [sum(widths[:n + 1]) for n in range(len(widths))]
        bb, w1_sb, w2_sb, diag_sb, w1_t, b1_sb, b2_sb = (columns_sb[:, e - w:e] for w, e in zip(widths, ends))
        gamma_sb = lines_sb[:, 0:D]
        beta_sb = lines_sb[:, D:2 * D]
        par_sb = lines_sb[:, 2 * D:2 * D + 4]
        t_sb = lines_sb[:, 2 * D + 4:2 * D + 5]
        zeros = scratch[:, stage_at + 2 * P:stage_at + 2 * P + BANK // 2].bitcast(BF16)
        xb = scratch[:, 0:CHUNKS * BANK]
        work = scratch[:, CHUNKS * BANK:(CHUNKS + 1) * BANK]
        th = scratch[:, (CHUNKS + 1) * BANK:(CHUNKS + 2) * BANK]
        xb_stage = scratch[:, (CHUNKS + 2) * BANK:(CHUNKS + 2) * BANK + SLOTS * HALVES * D]
        norm_at = (CHUNKS + 2) * BANK + SLOTS * HALVES * D
        stats = scratch[:, norm_at:norm_at + ROWS8 * 6]
        moments = scratch[:, norm_at + ROWS8 * 6:norm_at + ROWS8 * 8]
        deviation = scratch[:, norm_at + ROWS8 * 8:norm_at + ROWS8 * 9]
        inverse = scratch[:, norm_at + ROWS8 * 9:norm_at + ROWS8 * 10]
        xt = ring[:, 3 * PANEL:3 * PANEL + CHUNKS * BANK]

        def chunk(tile, c):
            return tile[:, c * BANK:(c + 1) * BANK]

        def rows(ap):
            return ap.rearrange("p (k d) -> p k d", d=D)

        def e_tile(c, t, h):
            at = c * BANK + (t * HALVES + h) * D
            return e_ht[:, at:at + D]

        def turned(r, h):
            at = stage_at + (r % STAGES) * GROUP + h * HALVES * P
            return scratch[:, at:at + HALVES * P]

        def turn_bank(r, h):
            return (bank_v if r % 2 else bank_a)[:, h * HALVES * P:(h + 1) * HALVES * P]

        def loaded_pair(m):
            return scratch[:, m * 2 * GROUP:(m + 1) * 2 * GROUP]

        def loaded(i, h):
            at = i * GROUP + h * HALVES * P
            return scratch[:, at:at + HALVES * P]

        def sum_column(c, t, h):
            return (c * TILES + t) * HALVES + h

        def tanh_part(n):
            return (work if n % 2 else th)[:, :]

        yt_ps = bank_y[:, 0:HALVES * P]
        y_ps = bank_y[:, HALVES * P:HALVES * P + HALVES * D]

        x_loaded = sem("x_loaded")
        small_loaded = sem("small_loaded")
        landed = [[sem(f"landed_{s}_{c}") for c in range(CHUNKS)] for s in range(SLOTS)]
        rows_landed = [sem(f"rows_landed_{m}") for m in range(PAIRS)]
        rows_used = sem("rows_used")
        rows_summed = sem("rows_summed")
        ident_ready = sem("ident_ready")
        zeros_ready = sem("zeros_ready")
        scale_step = sem("scale_step")
        x_turned = sem("x_turned")
        xt_copied = sem("xt_copied")
        xw_ready = sem("xw_ready")
        xw_scaled = sem("xw_scaled")
        e_ready = sem("e_ready")
        x2_step = sem("x2_step")
        act_turned = sem("act_turned")
        dve_turned = sem("dve_turned")
        act_copied = sem("act_copied")
        dve_copied = sem("dve_copied")
        first_done = sem("first_done")
        yt_copied = sem("yt_copied")
        y_summed = sem("y_summed")
        y_copied = sem("y_copied")
        second_done = sem("second_done")
        rowsum_ready = sem("rowsum_ready")
        ht_copied = sem("ht_copied")
        h_turned = sem("h_turned")
        stats_ready = sem("stats_ready")
        moments_ready = sem("moments_ready")
        deviation_ready = sem("deviation_ready")
        inverse_ready = sem("inverse_ready")
        normed = sem("normed")
        gamma_step = sem("gamma_step")
        x1_turned = sem("x1_turned")
        x1t_copied = sem("x1t_copied")
        xb_ready = sem("xb_ready")
        xb_copied = sem("xb_copied")
        xb_staged = sem("xb_staged")
        third_done = sem("third_done")
        hidden_ready = sem("hidden_ready")
        tanh_ready = sem("tanh_ready")
        mlp_done = sem("mlp_done")
        scaled_xb = sem("scaled_xb")
        base_ready = sem("base_ready")
        ut_copied = sem("ut_copied")
        u_turned = sem("u_turned")
        z_ready = sem("z_ready")
        stored = sem("stored")

        block = ctx.enter_context(nc.Block())

        @block.sync
        def _(sp):
            sp.dma_start(xrow[:, :], x).then_inc(x_loaded, 16)

            def load(panel, slot, c):
                at = slot * PANEL + c * PIECE
                sp.dma_start(ring[:, at:at + PIECE], adj[bass.ds((panel * CHUNKS + c) * P, P), :]
                             ).then_inc(landed[slot][c], 16)

            for slot in range(SLOTS):
                if slot > 1:
                    sp.wait_ge(rows_used, PAIRS * (slot - 1))
                for c in range(CHUNKS):
                    load(slot, slot, c)
            with sp.Fori(1, CHUNKS) as k:
                for slot in range(SLOTS):
                    for c in range(CHUNKS):
                        sp.wait_ge(second_done, k * (SLOTS * CHUNKS)
                                   + ((slot - SLOTS) * CHUNKS + CHUNK_ORDER.index(c) + 1))
                        load(k * SLOTS + slot, slot, c)
            with sp.Fori(0, CHUNKS - 1) as k:
                for slot in range(SLOTS):
                    for c in range(CHUNKS):
                        sp.wait_ge(third_done, k * (SLOTS * CHUNKS) + (slot * CHUNKS + c + 1))
                        load(k * SLOTS + slot, slot, c)
            for c in range(CHUNKS):
                sp.wait_ge(normed, 2 * CHUNKS + c + 1)
                sp.dma_start(out[:, c * BANK:(c + 1) * BANK], chunk(xrow, c)).then_inc(stored, 16)
            sp.wait_ge(stored, 16 * CHUNKS)

        @block.gpsimd
        def _(pool):
            def load_rows(panel, m):
                pool.dma_start(loaded_pair(m), adj_rows[bass.ds((panel * PAIRS + m) * P, P), :]
                               ).then_inc(rows_landed[m], 16)

            nc.gpsimd.memset(ident[:, :], 0.0).then_inc(ident_ready, 1)
            pool.wait_ge(ident_ready, 1)
            nc.gpsimd.affine_select(out=ident[:, :], in_=ident[:, :], compare_op=ALU.not_equal, fill=1.0,
                                    base=0, pattern=[[-1, P]], channel_multiplier=1).then_inc(ident_ready, 1)
            pool.wait_ge(ident_ready, 2)
            nc.gpsimd.tensor_tensor(stacked[:, :], ident[:, 0:D], ident[:, D:P], ALU.add).then_inc(ident_ready, 1)
            for m in range(PAIRS):
                load_rows(0, m)
            pool.wait_ge(e_ready, CHUNKS)
            nc.gpsimd.tensor_tensor(xrow[:, :], xrow[:, :], xrow[:, :], ALU.add).then_inc(x2_step, 1)
            pool.wait_ge(x2_step, 1)
            tiles = GROUPS * HALVES
            nc.gpsimd.tensor_tensor(rows(xrow[:, :]), rows(xrow[:, :]),
                                    beta_sb[:, :].unsqueeze(1).to_broadcast([P, tiles, D]),
                                    ALU.add).then_inc(x2_step, 1)
            pool.wait_ge(x2_step, 2)
            with pool.Fori(1, PANELS) as n:
                for m in range(PAIRS):
                    pool.wait_ge(rows_used, n * PAIRS + (m + 1 - PAIRS))
                    pool.wait_ge(rows_summed, n * PAIRS + (m + 1 - PAIRS))
                    load_rows(n, m)
            with pool.Fori(0, CHUNKS - 1) as k:
                for slot in range(SLOTS):
                    pool.wait_ge(third_done, k * (SLOTS * CHUNKS) + (slot + 1) * CHUNKS)
                    pool.wait_ge(xb_copied, k + 2)
                    nc.gpsimd.tensor_copy(
                        xb_stage[:, slot * HALVES * D:(slot + 1) * HALVES * D],
                        xb[:, bass.ds(k * BANK + slot * HALVES * D, HALVES * D)]).then_inc(xb_staged, 1)
            pool.wait_ge(rowsum_ready, 1)
            pool.wait_ge(x1_turned, CHUNKS)
            pool.wait_ge(xb_staged, SLOTS * (CHUNKS - 1))
            for c in range(CHUNKS):
                nc.gpsimd.tensor_tensor(
                    rows(chunk(xb, c)), rows(chunk(xb, c)),
                    rowsum[:, c * ROWS8:(c + 1) * ROWS8].unsqueeze(2).to_broadcast([P, ROWS8, D]),
                    ALU.mult).then_inc(scaled_xb, 1)
                pool.wait_ge(scaled_xb, c + 1)
                nc.gpsimd.tensor_tensor(chunk(xrow, c), chunk(xrow, c), chunk(xb, c),
                                        ALU.subtract).then_inc(base_ready, 1)

        @block.scalar
        def _(act):
            act.dma_start(matrices_sb[:, :], matrices).then_inc(small_loaded, 16)
            act.dma_start(columns_sb[:, :], columns).then_inc(small_loaded, 16)
            act.dma_start(lines_sb[:, :], lines.partition_broadcast(P)).then_inc(small_loaded, 16)
            act.wait_ge(zeros_ready, 1)
            nc.scalar.activation(table_warm[:, 0:1], eps_sb[:, 0:1], ACT.Sqrt)
            for c in range(CHUNKS):
                act.wait_ge(x_turned, c + 1)
                nc.scalar.copy(chunk(xt, c), acc[:, c, :]).then_inc(xt_copied, 1)
            with act.Fori(0, PANELS) as n:
                for r in range(0, len(TURNED), 2):
                    act.wait_ge(act_turned, n * SEGMENTS + (r // 2 + 1))
                    for h in range(HALVES):
                        last = nc.scalar.activation(
                            turned(r, h), turn_bank(r, h), ACT.Copy,
                            accum_out=sums_part[:, bass.ds(n * (GROUPS * HALVES) + sum_column(*TURNED[r], h), 1)])
                    last.then_inc(act_copied, 1)
            for q, c in enumerate(CHUNK_ORDER):
                act.wait_ge(second_done, (PANELS - 1) * CHUNKS + q + 1)
                nc.scalar.copy(chunk(e_ht, c), acc[:, c, :]).then_inc(ht_copied, 1)
            for q, c in enumerate(CHUNK_ORDER):
                for layer in range(2):
                    act.wait_ge(moments_ready, 2 * q + layer + 1)
                    nc.scalar.activation(deviation[:, :], moments[:, 1:2 * ROWS8:2], ACT.Sqrt,
                                         bias=eps_sb[:, 0:1]).then_inc(deviation_ready, 1)
                act.wait_ge(x1_turned, q + 1)
                nc.scalar.copy(chunk(e_ht, c), bank_v[:, :]).then_inc(x1t_copied, 1)
                act.wait_ge(xb_ready, q + 1)
                nc.scalar.copy(chunk(xb, c), bank_y[:, :]).then_inc(xb_copied, 1)
            for n in range(CHUNKS * HALVES):
                act.wait_ge(hidden_ready, n + 1)
                if n >= 2:
                    act.wait_ge(mlp_done, n - 1)
                nc.scalar.activation(tanh_part(n),
                                     (bank_y if n % 2 else bank_v)[:, :], ACT.Tanh,
                                     bias=b1_t[:, 0:1]).then_inc(tanh_ready, 1)
            nc.scalar.activation(table_warm[:, 1:2], eps_sb[:, 0:1], ACT.Sqrt)
            for c in range(CHUNKS):
                act.wait_ge(third_done, (PANELS - 1) * CHUNKS + c + 1)
                nc.scalar.activation(chunk(e_ht, c), acc[:, c, :], ACT.Identity,
                                     bias=b2_sb[:, 0:1]).then_inc(ut_copied, 1)
                if c > 0:
                    act.wait_ge(moments_ready, 2 * CHUNKS + c)
                    nc.scalar.activation(deviation[:, :], moments[:, 1:2 * ROWS8:2], ACT.Sqrt,
                                         bias=eps_sb[:, 0:1]).then_inc(deviation_ready, 1)
            act.wait_ge(moments_ready, 3 * CHUNKS)
            nc.scalar.activation(deviation[:, :], moments[:, 1:2 * ROWS8:2], ACT.Sqrt,
                                 bias=eps_sb[:, 0:1]).then_inc(deviation_ready, 1)

        @block.vector
        def _(dve):
            nc.vector.memset(zeros[:, :], 0.0)
            nc.vector.memset(eps_sb[:, :], EPS).then_inc(zeros_ready, 1)
            dve.wait_ge(small_loaded, 3 * 16)
            nc.vector.tensor_tensor(par_prod[:, 0:2], par_sb[:, 0:4:2], par_sb[:, 1:4:2],
                                    ALU.mult).then_inc(scale_step, 1)
            dve.wait_ge(scale_step, 1)
            nc.vector.tensor_scalar(scale[:, :], diag_sb[:, :], par_prod[:, 1:2], None,
                                    ALU.mult).then_inc(scale_step, 1)
            dve.wait_ge(scale_step, 2)
            users = USER_CHUNKS * ROWS8
            nc.vector.tensor_scalar(scale[:, 0:users:HALVES], diag_sb[:, 0:users:HALVES], par_prod[:, 0:1], None,
                                    ALU.mult).then_inc(scale_step, 1)
            nc.vector.scalar_tensor_tensor(out=b1_t[:, :], in0=w1_t[:, :], scalar=t_sb[:, 0:1], in1=b1_sb[:, :],
                                           op0=ALU.mult, op1=ALU.add).then_inc(scale_step, 1)
            dve.wait_ge(scale_step, 4)
            dve.wait_ge(x_loaded, 16)
            for c in range(CHUNKS):
                dve.wait_ge(xw_ready, c + 1)
                nc.vector.tensor_tensor(
                    rows(chunk(e_ht, c)), rows(acc[:, c, :]),
                    scale[:, c * ROWS8:(c + 1) * ROWS8].unsqueeze(2).to_broadcast([P, ROWS8, D]),
                    ALU.mult).then_inc(xw_scaled, 1)
                dve.wait_ge(xw_scaled, c + 1)
                nc.vector.tensor_tensor(chunk(e_ht, c), chunk(e_ht, c), chunk(xrow, c),
                                        ALU.add).then_inc(e_ready, 1)
            with dve.Fori(0, PANELS) as n:
                for r in range(1, len(TURNED), 2):
                    dve.wait_ge(dve_turned, n * SEGMENTS + (r // 2 + 1))
                    for h in range(HALVES):
                        last = nc.vector.tensor_scalar(
                            turned(r, h), turn_bank(r, h), 1.0, None, ALU.mult, ALU.add,
                            accum_out=sums_part[:, bass.ds(n * (GROUPS * HALVES) + sum_column(*TURNED[r], h), 1)])
                    last.then_inc(dve_copied, 1)
                    if r // 2 in SUMS_IN:
                        m = SUMS_IN.index(r // 2)
                        dve.wait_ge(rows_landed[m], n * 16 + 16)
                        nc.vector.tensor_reduce(
                            sums_part[:, bass.ds(n * (GROUPS * HALVES) + sum_column(*LOADED[2 * m], 0), 2 * HALVES)],
                            loaded_pair(m).rearrange("p (k j) -> p k j", j=HALVES * P),
                            AX.X, ALU.add).then_inc(rows_summed, 1)
                dve.wait_ge(first_done, n + 1)
                nc.vector.tensor_copy(yt_sb[:, :], yt_ps).then_inc(yt_copied, 1)
                dve.wait_ge(y_summed, n + 1)
                nc.vector.tensor_copy(y_sb[:, :], y_ps).then_inc(y_copied, 1)

            def inverse_deviations(src, n):
                for k in range(ROWS8):
                    last = nc.vector.bn_stats(stats[:, k * 6:(k + 1) * 6], src[:, k * D:(k + 1) * D])
                last.then_inc(stats_ready, 1)
                dve.wait_ge(stats_ready, n + 1)
                for k in range(ROWS8):
                    last = nc.vector.bn_aggr(moments[:, k * 2:(k + 1) * 2], stats[:, k * 6:(k + 1) * 6])
                last.then_inc(moments_ready, 1)
                dve.wait_ge(deviation_ready, n + 1)
                nc.vector.reciprocal(inverse[:, :], deviation[:, :]).then_inc(inverse_ready, 1)
                dve.wait_ge(inverse_ready, n + 1)

            def normalise(dst, src):
                for k in range(ROWS8):
                    last = nc.vector.tensor_scalar(dst[:, k * D:(k + 1) * D], src[:, k * D:(k + 1) * D],
                                                   moments[:, 2 * k:2 * k + 1], inverse[:, k:k + 1],
                                                   ALU.subtract, ALU.mult)
                last.then_inc(normed, 1)

            dve.wait_ge(x2_step, 2)
            for q, c in enumerate(CHUNK_ORDER):
                dve.wait_ge(h_turned, q + 1)
                inverse_deviations(bank_a, 2 * q)
                normalise(work, bank_a)
                dve.wait_ge(normed, 2 * q + 1)
                nc.vector.tensor_tensor(rows(work), rows(work),
                                        gamma_sb[:, :].unsqueeze(1).to_broadcast([P, ROWS8, D]),
                                        ALU.mult).then_inc(gamma_step, 1)
                dve.wait_ge(gamma_step, 2 * q + 1)
                nc.vector.tensor_tensor(work, work, chunk(xrow, c), ALU.add).then_inc(gamma_step, 1)
                dve.wait_ge(gamma_step, 2 * q + 2)
                inverse_deviations(work, 2 * q + 1)
                normalise(chunk(xrow, c), work)
                dve.wait_ge(normed, 2 * q + 2)
                if q == 0:
                    dve.wait_ge(act_copied, PANELS * SEGMENTS)
                    nc.vector.tensor_reduce(
                        rowsum[:, :], sums_part[:, :].rearrange("p (n k) -> p k n", n=PANELS),
                        AX.X, ALU.add).then_inc(rowsum_ready, 1)
            for c in range(CHUNKS):
                dve.wait_ge(u_turned, c + 1)
                dve.wait_ge(base_ready, c + 1)
                nc.vector.tensor_tensor(chunk(xrow, c), (bank_a, bank_v, bank_y)[c % 3][:, :], chunk(xrow, c),
                                        ALU.add).then_inc(z_ready, 1)
                dve.wait_ge(z_ready, c + 1)
                inverse_deviations(chunk(xrow, c), 2 * CHUNKS + c)
                normalise(chunk(xrow, c), chunk(xrow, c))
                dve.wait_ge(normed, 2 * CHUNKS + c + 1)

        @block.tensor
        def _(pe):
            def turn_chunk(bank, tile, c, done):
                for t in range(TILES):
                    at = c * BANK + t * P
                    last = pe.transpose(bank[:, t * P:(t + 1) * P], tile[:, at:at + P], ident[:, :])
                last.then_inc(done, 1)

            def times_blocks(bank, tile_t, c, blocks, done):
                for t in range(TILES):
                    at = c * BANK + t * P
                    last = pe.matmul(bank[:, t * P:(t + 1) * P], tile_t[:, at:at + P], blocks[:, :],
                                     start=True, stop=True)
                last.then_inc(done, 1)

            pe.wait_ge(x_loaded, 16)
            pe.wait_ge(ident_ready, 3)
            for c in range(CHUNKS):
                turn_chunk(acc[:, c, :], xrow, c, x_turned)
            pe.wait_ge(small_loaded, 3 * 16)
            pe.wait_ge(zeros_ready, 1)
            for c in range(CHUNKS):
                pe.wait_ge(xt_copied, c + 1)
                times_blocks(acc[:, c, :], xt, c, w_ui if c < USER_CHUNKS else w_ii, xw_ready)
            for c in range(CHUNKS):
                pe.wait_ge(xw_scaled, c + 1)
                last = pe.matmul(acc[:, c, :], zeros[:, 0:P], zeros[:, :], start=True, stop=False,
                                 skip_group_check=True)
            pe.wait_ge(e_ready, CHUNKS)

            def turn_group(k, u, r):
                c, t = TURNED[r]
                if t == 0:
                    pe.wait_ge(landed[u][c], k * 16 + 16)
                for h in range(HALVES):
                    for f in range(HALVES):
                        last = pe.transpose(turn_bank(r, h)[:, f * P:(f + 1) * P],
                                            piece(u, c, f, h)[:, t * P:(t + 1) * P], ident[:, :])
                last.then_inc(dve_turned if r % 2 else act_turned, 1)

            def first_product(group, rows_of, start=False, stop=False):
                for h in range(HALVES):
                    last = pe.matmul(yt_ps[h * D:(h + 1) * D, :], e_tile(*group, h), rows_of(h),
                                     start=start, stop=stop)
                return last

            def first_turned(k, u, r):
                pe.wait_ge(dve_copied if r % 2 else act_copied, k * (SLOTS * SEGMENTS) + (u * SEGMENTS + r // 2 + 1))
                last = first_product(TURNED[r], lambda h: turned(r, h), stop=(r == len(TURNED) - 1))
                if r == len(TURNED) - 1:
                    last.then_inc(first_done, 1)

            def first_loaded(k, u, i):
                if i % 2 == 0:
                    pe.wait_ge(rows_landed[i // 2], k * (16 * SLOTS) + 16 * (u + 1))
                last = first_product(LOADED[i], lambda h: loaded(i, h), start=(i == 0))
                if i % 2 == 1:
                    last.then_inc(rows_used, 1)

            def second_product(k, u, part):
                c, f = CHUNK_ORDER[part // HALVES], part % HALVES
                if part == 0:
                    pe.wait_ge(y_copied, k * SLOTS + (u + 1))
                if f == 0 and c in {c for c, _ in LOADED}:
                    pe.wait_ge(landed[u][c], k * 16 + 16)
                for h in range(HALVES):
                    last = pe.matmul(acc[h * D:(h + 1) * D, c, :], y_sb[:, f * D:(f + 1) * D], piece(u, c, f, h),
                                     start=False, stop=False, skip_group_check=True)
                if f == HALVES - 1:
                    last.then_inc(second_done, 1)

            def sum_y(k, u):
                pe.wait_ge(yt_copied, k * SLOTS + (u + 1))
                for f in range(HALVES):
                    last = pe.matmul(y_ps[:, f * D:(f + 1) * D], yt_sb[:, f * P:(f + 1) * P], stacked[:, :],
                                     start=True, stop=True)
                last.then_inc(y_summed, 1)

            with pe.Fori(0, CHUNKS) as k:
                for u in range(SLOTS):
                    part = i = 0
                    for segment in range(SEGMENTS):
                        turn_group(k, u, 2 * segment)
                        turn_group(k, u, 2 * segment + 1)
                        for _ in range(SECOND_IN[segment] if u > 0 else 0):
                            second_product(k, u - 1, part)
                            part += 1
                        for _ in range(LOADED_IN[segment]):
                            first_loaded(k, u, i)
                            i += 1
                        first_turned(k, u, 2 * segment)
                        first_turned(k, u, 2 * segment + 1)
                    while u > 0 and part < CHUNKS * HALVES:
                        second_product(k, u - 1, part)
                        part += 1
                    sum_y(k, u)
                for part in range(CHUNKS * HALVES):
                    second_product(k, SLOTS - 1, part)

            def third_product(u, weights, c, first=False):
                for f in range(HALVES):
                    for h in range(HALVES):
                        last = pe.matmul(acc[h * D:(h + 1) * D, c, :], weights[:, f * D:(f + 1) * D],
                                         piece(u, c, f, h), start=(first and f == 0), stop=False,
                                         skip_group_check=True)
                last.then_inc(third_done, 1)

            pe.wait_ge(ht_copied, 1)
            turn_chunk(bank_a, e_ht, CHUNK_ORDER[0], h_turned)
            for q, c in enumerate(CHUNK_ORDER):
                if q > 0:
                    if q == 1:
                        pe.wait_ge(ht_copied, CHUNKS)
                        pe.wait_ge(xb_copied, 1)
                    at = CHUNK_ORDER[0] * BANK + (q - 1) * HALVES * D
                    for b in range(CHUNKS):
                        third_product(q - 1, xb[:, at:at + HALVES * D], b, first=(q == 1))
                pe.wait_ge(normed, 2 * q + 2)
                if q > 0:
                    pe.wait_ge(x1t_copied, q)
                turn_chunk(bank_v, xrow, c, x1_turned)
                if q + 1 < CHUNKS:
                    pe.wait_ge(ht_copied, q + 2)
                    turn_chunk(bank_a, e_ht, CHUNK_ORDER[q + 1], h_turned)
                pe.wait_ge(x1t_copied, q + 1)
                if q > 0:
                    pe.wait_ge(xb_copied, q)
                times_blocks(bank_y, e_ht, c, bb, xb_ready)

            def hidden(n):
                c, h = divmod(n, HALVES)
                if n >= 2:
                    pe.wait_ge(tanh_ready, n - 1)
                elif n == 1:
                    pe.wait_ge(xb_copied, CHUNKS)
                pe.matmul((bank_y if n % 2 else bank_v)[:, :], w1_sb[h * D:(h + 1) * D, :],
                          e_ht[h * D:(h + 1) * D, c * BANK:(c + 1) * BANK],
                          start=True, stop=True).then_inc(hidden_ready, 1)

            hidden(0)
            for n in range(CHUNKS * HALVES):
                c, h = divmod(n, HALVES)
                if n + 1 < CHUNKS * HALVES:
                    hidden(n + 1)
                pe.wait_ge(tanh_ready, n + 1)
                pe.matmul(acc[h * D:(h + 1) * D, c, :], w2_sb[:, :], tanh_part(n),
                          start=False, stop=False, skip_group_check=True).then_inc(mlp_done, 1)

            def third_of_loaded(k, u, last=False):
                pe.wait_ge(xb_staged, k * SLOTS + (u + 1))
                for c in range(CHUNKS):
                    pe.wait_ge(landed[u][c], k * 16 + 16 * (CHUNKS + 1))
                    third_product(u, xb_stage[:, u * HALVES * D:(u + 1) * HALVES * D], c)
                    if last and c > 0:
                        turn_u(c - 1)

            def turn_u(c):
                pe.wait_ge(ut_copied, c + 1)
                if c >= 3:
                    pe.wait_ge(z_ready, c - 2)
                turn_chunk((bank_a, bank_v, bank_y)[c % 3], e_ht, c, u_turned)

            with pe.Fori(0, CHUNKS - 2) as k:
                for u in range(SLOTS):
                    third_of_loaded(k, u)
            for u in range(SLOTS):
                third_of_loaded(CHUNKS - 2, u, last=(u == SLOTS - 1))
            turn_u(CHUNKS - 1)


def kernel(x, adj, L0_gnn_W_u, L0_gnn_diag_u, L0_gnn_par_u, L0_gnn_W_i, L0_gnn_diag_i, L0_gnn_par_i,
           L0_gnn_ln_gamma, L0_gnn_ln_beta, L1_gnn_t, L1_gnn_B, L1_gnn_W1, L1_gnn_b1, L1_gnn_W2, L1_gnn_b2):
    import numpy as np
    import concourse.bacc as bacc
    from concourse.bass_utils import run_bass_kernel_spmd

    nc = bacc.Bacc("TRN2", target_bir_lowering=False, num_devices=1)
    def blocks(a, b):
        m = np.zeros((P, P), np.float32)
        m[0:D, 0:D], m[D:P, D:P] = a, b
        return m

    w1 = np.asarray(L1_gnn_W1)
    a6 = np.asarray(adj).reshape(HALVES, CHUNKS, BANK, HALVES, CHUNKS, TILES, P)
    laid = {
        "adj": a6.transpose(4, 5, 1, 6, 3, 0, 2).reshape(PANELS * CHUNKS * P, PIECE),
        "adj_rows": np.asarray(adj).reshape(HALVES, CHUNKS, 2, 2, P, HALVES, PANELS, P)
        [:, sorted({c for c, _ in LOADED})].transpose(6, 1, 2, 4, 3, 0, 5, 7).reshape(PANELS * PAIRS * P, 2 * GROUP),
        "x": np.asarray(x).reshape(HALVES, CHUNKS, TILES, P, D).transpose(3, 1, 2, 0, 4).reshape(P, CHUNKS * BANK),
        "matrices": np.concatenate([blocks(L0_gnn_W_u, L0_gnn_W_i), blocks(L0_gnn_W_i, L0_gnn_W_i)], axis=1),
        "columns": np.concatenate([
            blocks(np.asarray(L1_gnn_B).T, np.asarray(L1_gnn_B).T), np.tile(w1[0:D], (HALVES, 1)), L1_gnn_W2,
            np.concatenate([L0_gnn_diag_u, L0_gnn_diag_i]).reshape(HALVES, CHUNKS, TILES, P)
            .transpose(3, 1, 2, 0).reshape(P, GROUPS * HALVES),
            w1[D].reshape(P, 1), np.asarray(L1_gnn_b1).reshape(P, 1),
            np.tile(np.asarray(L1_gnn_b2).reshape(D, 1), (HALVES, 1))], axis=1),
        "lines": np.concatenate([L0_gnn_ln_gamma, L0_gnn_ln_beta, L0_gnn_par_u, L0_gnn_par_i, L1_gnn_t]),
    }
    arrays, args = {}, {}
    for name, a in laid.items():
        a = np.ascontiguousarray(a)
        arrays["in_" + name] = a
        args[name] = nc.dram_tensor("in_" + name, a.shape, mybir.dt.from_np(a.dtype), kind="ExternalInput").ap()
    args["out"] = nc.dram_tensor("out_rows", (P, CHUNKS * BANK), F32, kind="ExternalOutput").ap()
    gnn_kernel(nc, **args)
    r = run_bass_kernel_spmd(nc, [arrays], core_ids=[0])
    got = r.results[0]["out_rows"].reshape(P, CHUNKS, TILES, HALVES, D).transpose(3, 1, 2, 0, 4)
    return np.ascontiguousarray(got.reshape(N, D))
```

```python
from contextlib import ExitStack

import concourse.bass as bass
from concourse import mybir

F32 = mybir.dt.float32
BF16 = mybir.dt.bfloat16
ALU = mybir.AluOpType
ACT = mybir.ActivationFunctionType
AX = mybir.AxisListType

P = 128
D = 64
N = 5120
HALVES = 2
CHUNKS = 5
TILES = 4
BANK = TILES * P
ROWS8 = TILES * HALVES
HIDDEN = 128
N_USERS = 2048
USER_CHUNKS = N_USERS // BANK
PANELS = CHUNKS * TILES
SLOTS = TILES
GROUPS = CHUNKS * TILES
PIECE = HALVES * HALVES * BANK
PANEL = CHUNKS * PIECE
STAGES = 2
GROUP = HALVES * HALVES * P
BUFFERS = 4
ROUNDS = PANELS // SLOTS
EPS = 1e-5

CHUNK_ORDER = [CHUNKS - 1] + list(range(CHUNKS - 1))
BATCHES = [(CHUNKS - 1, 0, 1), (CHUNKS - 1, 1, TILES)] + [(c, 0, TILES) for c in range(CHUNKS - 1)]
NORMS = 2 * len(BATCHES)


def spread(count, parts):
    return [count * (n + 1) // parts - count * n // parts for n in range(parts)]


class Plan:

    def __init__(self, loaded_pairs):
        self.loaded_pairs = loaded_pairs
        self.loaded = [(c, t + i) for c, t in loaded_pairs for i in range(2)]
        self.turned = [(c, t) for c in range(CHUNKS) for t in range(TILES) if (c, t) not in self.loaded]
        self.pairs = len(loaded_pairs)
        self.segments = len(self.turned) // 2
        self.loaded_in = spread(len(self.loaded), self.segments)
        self.second_in = spread(CHUNKS * HALVES - 2, self.segments)
        self.sums_in = spread(self.pairs, self.segments)
        pieces = dict.fromkeys([c for c, _ in self.turned] + CHUNK_ORDER)
        at = [(n / CHUNKS, "piece", c) for n, c in enumerate(pieces)]
        at += [((m + 0.5) / self.pairs, "pair", m) for m in range(self.pairs)]
        self.loads = [(kind, n) for _, kind, n in sorted(at)]


def pairs_but(*tiles):
    return [(c, t) for c in range(CHUNKS) for t in (0, 2) if (c, t) not in tiles]


FIRST = Plan(pairs_but((0, 0), (0, 2), (2, 0), (2, 2), (4, 0)))
LATER = Plan(pairs_but((0, 0), (0, 2), (2, 0), (2, 2)))


def plan_of(k):
    return FIRST if isinstance(k, int) and k == 0 else LATER


def count_at(k, u, per_panel, more=0):
    more += u * per_panel(plan_of(k))
    if isinstance(k, int) and k == 0:
        return more
    return k * (SLOTS * per_panel(LATER)) + (SLOTS * (per_panel(FIRST) - per_panel(LATER)) + more)


def pairs_of(plan):
    return plan.pairs


def segments_of(plan):
    return plan.segments


def gnn_kernel(nc, adj, adj_rows, x, matrices, columns, lines, out):
    with ExitStack() as ctx:
        def sb(name, shape, dt=F32):
            return ctx.enter_context(nc.sbuf_tensor(name, shape, dt))

        def sem(name):
            return ctx.enter_context(nc.semaphore(name))

        ring = sb("ring", [P, SLOTS * PANEL])
        xrow = sb("xrow", [P, CHUNKS * BANK])
        e_ht = sb("e_ht", [P, CHUNKS * BANK])
        scratch = sb("scratch", [P, BUFFERS * 2 * GROUP + STAGES * GROUP])
        sums_part = sb("sums_part", [P, PANELS * GROUPS * HALVES])
        rowsum = sb("rowsum", [P, GROUPS * HALVES])
        ident = sb("ident", [P, P])
        stacked = sb("stacked", [P, D])
        columns_sb = sb("columns_sb", [P, columns.shape[1]])
        lines_sb = sb("lines_sb", [P, lines.shape[0]])
        par_prod = sb("par_prod", [P, 2])
        scale = sb("scale", [P, GROUPS * HALVES])
        b1_t = sb("b1_t", [P, 1])
        eps_sb = sb("eps_sb", [P, 1])
        table_warm = sb("table_warm", [P, 2])
        yt_sb = sb("yt_sb", [P, HALVES * P])
        y_sb = sb("y_sb", [P, HALVES * D])

        acc = ctx.enter_context(nc.psum_tensor("acc", [P, CHUNKS, BANK], F32))
        bank_a = ctx.enter_context(nc.psum_tensor("bank_a", [P, BANK], F32))
        bank_v = ctx.enter_context(nc.psum_tensor("bank_v", [P, BANK], F32))
        bank_y = ctx.enter_context(nc.psum_tensor("bank_y", [P, BANK], F32))

        def piece(slot, c, f, h):
            at = slot * PANEL + c * PIECE + (f * HALVES + h) * BANK
            return ring[:, at:at + BANK]

        stage_at = BUFFERS * 2 * GROUP
        matrices_sb = scratch[:, stage_at:stage_at + 2 * P]
        w_ui = matrices_sb[:, 0:P]
        w_ii = matrices_sb[:, P:2 * P]
        widths = [P, HIDDEN, D, GROUPS * HALVES, 1, 1, 1]
        ends = [sum(widths[:n + 1]) for n in range(len(widths))]
        bb, w1_sb, w2_sb, diag_sb, w1_t, b1_sb, b2_sb = (columns_sb[:, e - w:e] for w, e in zip(widths, ends))
        gamma_sb = lines_sb[:, 0:D]
        beta_sb = lines_sb[:, D:2 * D]
        par_sb = lines_sb[:, 2 * D:2 * D + 4]
        t_sb = lines_sb[:, 2 * D + 4:2 * D + 5]
        zeros = scratch[:, stage_at + 2 * P:stage_at + 2 * P + BANK // 2].bitcast(BF16)
        xb = scratch[:, 0:CHUNKS * BANK]
        work = scratch[:, CHUNKS * BANK:(CHUNKS + 1) * BANK]
        th = scratch[:, (CHUNKS + 1) * BANK:(CHUNKS + 2) * BANK]
        xb_stage = scratch[:, (CHUNKS + 2) * BANK:(CHUNKS + 2) * BANK + SLOTS * HALVES * D]
        norm_at = (CHUNKS + 2) * BANK + SLOTS * HALVES * D

        def norm_part(n, first, width):
            at = norm_at + (n % 2) * ROWS8 * 10 + first * ROWS8
            return scratch[:, at:at + width * ROWS8]

        def stats(n):
            return norm_part(n, 0, 6)

        def moments(n):
            return norm_part(n, 6, 2)

        def deviation(n):
            return norm_part(n, 8, 1)

        def inverse(n):
            return norm_part(n, 9, 1)

        xt = ring[:, 3 * PANEL:3 * PANEL + CHUNKS * BANK]

        def chunk(tile, c):
            return tile[:, c * BANK:(c + 1) * BANK]

        def rows(ap):
            return ap.rearrange("p (k d) -> p k d", d=D)

        def e_tile(c, t, h):
            at = c * BANK + (t * HALVES + h) * D
            return e_ht[:, at:at + D]

        def turned(r, h):
            at = stage_at + (r % STAGES) * GROUP + h * HALVES * P
            return scratch[:, at:at + HALVES * P]

        def turn_bank(r, h):
            return (bank_v if r % 2 else bank_a)[:, h * HALVES * P:(h + 1) * HALVES * P]

        def buffer(k, u, m):
            return (u * plan_of(k).pairs + m) % BUFFERS

        def rows_landings(k, u, m):
            return count_at(k, 0, lambda plan: plan.pairs * 16 // BUFFERS,
                            16 * ((u * plan_of(k).pairs + m) // BUFFERS + 1))

        def loaded_pair(k, u, m):
            at = buffer(k, u, m) * 2 * GROUP
            return scratch[:, at:at + 2 * GROUP]

        def loaded(k, u, i, h):
            at = (i % 2) * GROUP + h * HALVES * P
            return loaded_pair(k, u, i // 2)[:, at:at + HALVES * P]

        def sum_column(c, t, h):
            return (c * TILES + t) * HALVES + h

        def panel_sums(k, u, c, t, h, count):
            at = u * GROUPS * HALVES + sum_column(c, t, h)
            return sums_part[:, bass.ds(k * (SLOTS * GROUPS * HALVES) + at, count)]

        def tanh_part(n):
            return (work if n % 2 else th)[:, :]

        yt_ps = bank_y[:, 0:HALVES * P]
        y_ps = bank_y[:, HALVES * P:HALVES * P + HALVES * D]

        x_loaded = sem("x_loaded")
        small_loaded = sem("small_loaded")
        landed = [[sem(f"landed_{s}_{c}") for c in range(CHUNKS)] for s in range(SLOTS)]
        rows_landed = [sem(f"rows_landed_{m}") for m in range(BUFFERS)]
        rows_used = sem("rows_used")
        rows_summed = sem("rows_summed")
        ident_ready = sem("ident_ready")
        zeros_ready = sem("zeros_ready")
        scale_step = sem("scale_step")
        x_turned = sem("x_turned")
        xt_copied = sem("xt_copied")
        xw_ready = sem("xw_ready")
        xw_scaled = sem("xw_scaled")
        e_ready = sem("e_ready")
        x2_step = sem("x2_step")
        act_turned = sem("act_turned")
        dve_turned = sem("dve_turned")
        act_copied = sem("act_copied")
        dve_copied = sem("dve_copied")
        first_done = sem("first_done")
        yt_copied = sem("yt_copied")
        y_summed = sem("y_summed")
        y_copied = sem("y_copied")
        second_done = sem("second_done")
        rowsum_ready = sem("rowsum_ready")
        ht_copied = sem("ht_copied")
        h_turned = sem("h_turned")
        stats_ready = sem("stats_ready")
        moments_ready = sem("moments_ready")
        deviation_ready = sem("deviation_ready")
        inverse_ready = sem("inverse_ready")
        centred = sem("centred")
        normed = sem("normed")
        gamma_step = sem("gamma_step")
        x1_turned = sem("x1_turned")
        x1t_copied = sem("x1t_copied")
        xb_ready = sem("xb_ready")
        xb_copied = sem("xb_copied")
        xb_staged = sem("xb_staged")
        third_done = sem("third_done")
        hidden_ready = sem("hidden_ready")
        tanh_ready = sem("tanh_ready")
        mlp_done = sem("mlp_done")
        scaled_xb = sem("scaled_xb")
        base_ready = sem("base_ready")
        ut_copied = sem("ut_copied")
        u_turned = sem("u_turned")
        z_ready = sem("z_ready")
        z_centred = sem("z_centred")
        z_normed = sem("z_normed")
        stored = sem("stored")

        block = ctx.enter_context(nc.Block())

        @block.sync
        def _(sp):
            sp.dma_start(xrow[:, :], x).then_inc(x_loaded, 16)
            sp.dma_start(matrices_sb[:, :], matrices).then_inc(small_loaded, 16)
            sp.dma_start(columns_sb[:, :], columns).then_inc(small_loaded, 16)
            sp.dma_start(lines_sb[:, :], lines.partition_broadcast(P)).then_inc(small_loaded, 16)

            def load(panel, slot, c):
                at = slot * PANEL + c * PIECE
                sp.dma_start(ring[:, at:at + PIECE], adj[bass.ds((panel * CHUNKS + c) * P, P), :]
                             ).then_inc(landed[slot][c], 16)

            def load_rows(k, u, m):
                pair = count_at(k, u, pairs_of, m)
                if not isinstance(pair, int) or pair >= BUFFERS:
                    sp.wait_ge(rows_used, pair + (1 - BUFFERS))
                    sp.wait_ge(rows_summed, pair + (1 - BUFFERS))
                sp.dma_start(loaded_pair(k, u, m), adj_rows[bass.ds(pair * P, P), :]
                             ).then_inc(rows_landed[buffer(k, u, m)], 16)

            def load_piece(k, slot, c):
                if not isinstance(k, int) or k > 0:
                    sp.wait_ge(second_done, k * (SLOTS * CHUNKS)
                               + ((slot - SLOTS) * CHUNKS + CHUNK_ORDER.index(c) + 1))
                load(k * SLOTS + slot, slot, c)

            def round_of_loads(k):
                for u in range(SLOTS):
                    for kind, n in plan_of(k).loads:
                        if kind == "piece":
                            load_piece(k, u, n)
                        else:
                            load_rows(k, u, n)

            round_of_loads(0)
            with sp.Fori(1, ROUNDS) as k:
                round_of_loads(k)
            with sp.Fori(0, CHUNKS - 1) as k:
                for slot in range(SLOTS):
                    for c in range(CHUNKS):
                        sp.wait_ge(third_done, k * (SLOTS * CHUNKS) + (slot * CHUNKS + c + 1))
                        load(k * SLOTS + slot, slot, c)
            for c in range(CHUNKS):
                if c < CHUNKS - 1:
                    sp.wait_ge(z_normed, c + 1)
                else:
                    sp.wait_ge(normed, NORMS + 1)
                sp.dma_start(out[:, c * BANK:(c + 1) * BANK], chunk(xrow, c)).then_inc(stored, 16)
            sp.wait_ge(stored, 16 * CHUNKS)

        @block.gpsimd
        def _(pool):
            nc.gpsimd.memset(ident[:, :], 0.0).then_inc(ident_ready, 1)
            pool.wait_ge(ident_ready, 1)
            nc.gpsimd.affine_select(out=ident[:, :], in_=ident[:, :], compare_op=ALU.not_equal, fill=1.0,
                                    base=0, pattern=[[-1, P]], channel_multiplier=1).then_inc(ident_ready, 1)
            pool.wait_ge(ident_ready, 2)
            nc.gpsimd.tensor_tensor(stacked[:, :], ident[:, 0:D], ident[:, D:P], ALU.add).then_inc(ident_ready, 1)
            pool.wait_ge(e_ready, CHUNKS)
            nc.gpsimd.tensor_tensor(xrow[:, :], xrow[:, :], xrow[:, :], ALU.add).then_inc(x2_step, 1)
            pool.wait_ge(x2_step, 1)
            tiles = GROUPS * HALVES
            nc.gpsimd.tensor_tensor(rows(xrow[:, :]), rows(xrow[:, :]),
                                    beta_sb[:, :].unsqueeze(1).to_broadcast([P, tiles, D]),
                                    ALU.add).then_inc(x2_step, 1)
            pool.wait_ge(x2_step, 2)
            with pool.Fori(1, CHUNKS - 1) as k:
                for slot in range(SLOTS):
                    pool.wait_ge(third_done, k * (SLOTS * CHUNKS) + (slot + 1) * CHUNKS)
                    pool.wait_ge(xb_copied, k + 3)
                    nc.gpsimd.tensor_copy(
                        xb_stage[:, slot * HALVES * D:(slot + 1) * HALVES * D],
                        xb[:, bass.ds(k * BANK + slot * HALVES * D, HALVES * D)]).then_inc(xb_staged, 1)
            pool.wait_ge(rowsum_ready, 1)
            pool.wait_ge(x1_turned, len(BATCHES))
            pool.wait_ge(xb_staged, SLOTS * (CHUNKS - 2))
            for c in range(CHUNKS):
                nc.gpsimd.tensor_tensor(
                    rows(chunk(xb, c)), rows(chunk(xb, c)),
                    rowsum[:, c * ROWS8:(c + 1) * ROWS8].unsqueeze(2).to_broadcast([P, ROWS8, D]),
                    ALU.mult).then_inc(scaled_xb, 1)
                pool.wait_ge(scaled_xb, c + 1)
                nc.gpsimd.tensor_tensor(chunk(xrow, c), chunk(xrow, c), chunk(xb, c),
                                        ALU.subtract).then_inc(base_ready, 1)
            for c in range(CHUNKS - 1):
                n = NORMS + c
                pool.wait_ge(moments_ready, n + 1)
                nc.gpsimd.tensor_tensor(rows(chunk(xrow, c)), rows(chunk(xrow, c)),
                                        moments(n)[:, 0:2 * ROWS8:2].unsqueeze(2).to_broadcast([P, ROWS8, D]),
                                        ALU.subtract).then_inc(z_centred, 1)
                pool.wait_ge(z_centred, c + 1)
                pool.wait_ge(inverse_ready, n + 1)
                nc.gpsimd.tensor_tensor(rows(chunk(xrow, c)), rows(chunk(xrow, c)),
                                        inverse(n).unsqueeze(2).to_broadcast([P, ROWS8, D]),
                                        ALU.mult).then_inc(z_normed, 1)

        @block.scalar
        def _(act):
            act.wait_ge(zeros_ready, 1)
            nc.scalar.activation(table_warm[:, 0:1], eps_sb[:, 0:1], ACT.Sqrt)
            for c in range(CHUNKS):
                act.wait_ge(x_turned, c + 1)
                nc.scalar.copy(chunk(xt, c), acc[:, c, :]).then_inc(xt_copied, 1)
            def round_of_copies(k):
                plan = plan_of(k)
                for u in range(SLOTS):
                    for r in range(0, len(plan.turned), 2):
                        act.wait_ge(act_turned, count_at(k, u, segments_of, r // 2 + 1))
                        for h in range(HALVES):
                            last = nc.scalar.activation(turned(r, h), turn_bank(r, h), ACT.Copy,
                                                        accum_out=panel_sums(k, u, *plan.turned[r], h, 1))
                        last.then_inc(act_copied, 1)

            round_of_copies(0)
            with act.Fori(1, ROUNDS) as k:
                round_of_copies(k)
            def copy_ht(q):
                act.wait_ge(second_done, (PANELS - 1) * CHUNKS + q + 1)
                nc.scalar.copy(chunk(e_ht, CHUNK_ORDER[q]), acc[:, CHUNK_ORDER[q], :]).then_inc(ht_copied, 1)

            def square_root(n, tiles):
                act.wait_ge(moments_ready, n + 1)
                nc.scalar.activation(deviation(n)[:, 0:tiles], moments(n)[:, 1:2 * tiles:2], ACT.Sqrt,
                                     bias=eps_sb[:, 0:1]).then_inc(deviation_ready, 1)

            for b, (c, t0, t1) in enumerate(BATCHES):
                tiles = (t1 - t0) * HALVES
                if b == 0:
                    copy_ht(0)
                    square_root(0, tiles)
                    copy_ht(1)
                    copy_ht(2)
                    square_root(1, tiles)
                else:
                    square_root(2 * b, tiles)
                    square_root(2 * b + 1, tiles)
                act.wait_ge(x1_turned, b + 1)
                nc.scalar.copy(chunk(e_ht, c)[:, t0 * P:t1 * P], bank_v[:, t0 * P:t1 * P]).then_inc(x1t_copied, 1)
                if b == 0:
                    copy_ht(3)
                act.wait_ge(xb_ready, b + 1)
                nc.scalar.copy(chunk(xb, c)[:, t0 * P:t1 * P], bank_y[:, t0 * P:t1 * P]).then_inc(xb_copied, 1)
                if b == 0:
                    copy_ht(4)
            for n in range(CHUNKS * HALVES):
                act.wait_ge(hidden_ready, n + 1)
                if n >= 2:
                    act.wait_ge(mlp_done, n - 1)
                nc.scalar.activation(tanh_part(n),
                                     (bank_y if n % 2 else bank_v)[:, :], ACT.Tanh,
                                     bias=b1_t[:, 0:1]).then_inc(tanh_ready, 1)
            nc.scalar.activation(table_warm[:, 1:2], eps_sb[:, 0:1], ACT.Sqrt)
            for c in range(CHUNKS):
                act.wait_ge(third_done, (PANELS - 1) * CHUNKS + c + 1)
                nc.scalar.activation(chunk(e_ht, c), acc[:, c, :], ACT.Identity,
                                     bias=b2_sb[:, 0:1]).then_inc(ut_copied, 1)
                if c > 0:
                    square_root(NORMS + c - 1, ROWS8)
            square_root(NORMS + CHUNKS - 1, ROWS8)

        @block.vector
        def _(dve):
            nc.vector.memset(zeros[:, :], 0.0)
            nc.vector.memset(eps_sb[:, :], EPS).then_inc(zeros_ready, 1)
            dve.wait_ge(small_loaded, 3 * 16)
            nc.vector.tensor_tensor(par_prod[:, 0:2], par_sb[:, 0:4:2], par_sb[:, 1:4:2],
                                    ALU.mult).then_inc(scale_step, 1)
            dve.wait_ge(scale_step, 1)
            nc.vector.tensor_scalar(scale[:, :], diag_sb[:, :], par_prod[:, 1:2], None,
                                    ALU.mult).then_inc(scale_step, 1)
            dve.wait_ge(scale_step, 2)
            users = USER_CHUNKS * ROWS8
            nc.vector.tensor_scalar(scale[:, 0:users:HALVES], diag_sb[:, 0:users:HALVES], par_prod[:, 0:1], None,
                                    ALU.mult).then_inc(scale_step, 1)
            nc.vector.scalar_tensor_tensor(out=b1_t[:, :], in0=w1_t[:, :], scalar=t_sb[:, 0:1], in1=b1_sb[:, :],
                                           op0=ALU.mult, op1=ALU.add).then_inc(scale_step, 1)
            dve.wait_ge(scale_step, 4)
            dve.wait_ge(x_loaded, 16)
            for c in range(CHUNKS):
                dve.wait_ge(xw_ready, c + 1)
                nc.vector.tensor_tensor(
                    rows(chunk(e_ht, c)), rows(acc[:, c, :]),
                    scale[:, c * ROWS8:(c + 1) * ROWS8].unsqueeze(2).to_broadcast([P, ROWS8, D]),
                    ALU.mult).then_inc(xw_scaled, 1)
                dve.wait_ge(xw_scaled, c + 1)
                nc.vector.tensor_tensor(chunk(e_ht, c), chunk(e_ht, c), chunk(xrow, c),
                                        ALU.add).then_inc(e_ready, 1)
            def round_of_sums(k):
                plan = plan_of(k)
                for u in range(SLOTS):
                    m = 0
                    for segment in range(plan.segments):
                        for _ in range(plan.sums_in[segment]):
                            dve.wait_ge(rows_landed[buffer(k, u, m)], rows_landings(k, u, m))
                            nc.vector.tensor_reduce(
                                panel_sums(k, u, *plan.loaded_pairs[m], 0, 2 * HALVES),
                                loaded_pair(k, u, m).rearrange("p (k j) -> p k j", j=HALVES * P),
                                AX.X, ALU.add).then_inc(rows_summed, 1)
                            m += 1
                        r = 2 * segment + 1
                        if r < len(plan.turned):
                            dve.wait_ge(dve_turned, count_at(k, u, segments_of, segment + 1))
                            for h in range(HALVES):
                                last = nc.vector.tensor_scalar(
                                    turned(r, h), turn_bank(r, h), 1.0, None, ALU.mult, ALU.add,
                                    accum_out=panel_sums(k, u, *plan.turned[r], h, 1))
                            last.then_inc(dve_copied, 1)
                    dve.wait_ge(first_done, k * SLOTS + (u + 1))
                    nc.vector.tensor_copy(yt_sb[:, :], yt_ps).then_inc(yt_copied, 1)
                    dve.wait_ge(y_summed, k * SLOTS + (u + 1))
                    nc.vector.tensor_copy(y_sb[:, :], y_ps).then_inc(y_copied, 1)

            round_of_sums(0)
            with dve.Fori(1, ROUNDS) as k:
                round_of_sums(k)

            def inverse_deviations(src, n, tiles):
                for k in range(tiles):
                    last = nc.vector.bn_stats(stats(n)[:, k * 6:(k + 1) * 6], src[:, k * D:(k + 1) * D])
                last.then_inc(stats_ready, 1)
                dve.wait_ge(stats_ready, n + 1)
                for k in range(tiles):
                    last = nc.vector.bn_aggr(moments(n)[:, k * 2:(k + 1) * 2], stats(n)[:, k * 6:(k + 1) * 6])
                last.then_inc(moments_ready, 1)
                dve.wait_ge(deviation_ready, n + 1)
                nc.vector.reciprocal(inverse(n)[:, 0:tiles], deviation(n)[:, 0:tiles]).then_inc(inverse_ready, 1)

            def normalise(dst, src, n, tiles):
                at = min(n, NORMS) + 1
                dve.wait_ge(moments_ready, n + 1)
                nc.vector.tensor_tensor(rows(dst), rows(src),
                                        moments(n)[:, 0:2 * tiles:2].unsqueeze(2).to_broadcast([P, tiles, D]),
                                        ALU.subtract).then_inc(centred, 1)
                dve.wait_ge(centred, at)
                dve.wait_ge(inverse_ready, n + 1)
                nc.vector.tensor_tensor(rows(dst), rows(dst),
                                        inverse(n)[:, 0:tiles].unsqueeze(2).to_broadcast([P, tiles, D]),
                                        ALU.mult).then_inc(normed, 1)
                dve.wait_ge(normed, at)

            dve.wait_ge(x2_step, 2)
            for b, (c, t0, t1) in enumerate(BATCHES):
                tiles = (t1 - t0) * HALVES
                h_rows, z, x_rows = (a[:, t0 * P:t1 * P] for a in (bank_a, work, chunk(xrow, c)))
                dve.wait_ge(h_turned, max(b, 1))
                inverse_deviations(h_rows, 2 * b, tiles)
                normalise(z, h_rows, 2 * b, tiles)
                nc.vector.tensor_tensor(rows(z), rows(z), gamma_sb[:, :].unsqueeze(1).to_broadcast([P, tiles, D]),
                                        ALU.mult).then_inc(gamma_step, 1)
                dve.wait_ge(gamma_step, 2 * b + 1)
                nc.vector.tensor_tensor(z, z, x_rows, ALU.add).then_inc(gamma_step, 1)
                dve.wait_ge(gamma_step, 2 * b + 2)
                inverse_deviations(z, 2 * b + 1, tiles)
                normalise(x_rows, z, 2 * b + 1, tiles)
            dve.wait_ge(act_copied, count_at(ROUNDS - 1, SLOTS, segments_of))
            nc.vector.tensor_reduce(rowsum[:, :], sums_part[:, :].rearrange("p (n k) -> p k n", n=PANELS),
                                    AX.X, ALU.add).then_inc(rowsum_ready, 1)
            for c in range(CHUNKS):
                dve.wait_ge(u_turned, c + 1)
                dve.wait_ge(base_ready, c + 1)
                nc.vector.tensor_tensor(chunk(xrow, c), (bank_a, bank_v, bank_y)[c % 3][:, :], chunk(xrow, c),
                                        ALU.add).then_inc(z_ready, 1)
                dve.wait_ge(z_ready, c + 1)
                if c >= 2:
                    dve.wait_ge(z_normed, c - 1)
                inverse_deviations(chunk(xrow, c), NORMS + c, ROWS8)
            normalise(chunk(xrow, CHUNKS - 1), chunk(xrow, CHUNKS - 1), NORMS + CHUNKS - 1, ROWS8)

        @block.tensor
        def _(pe):
            def turn_chunk(bank, tile, c, done, t0=0, t1=TILES):
                for t in range(t0, t1):
                    at = c * BANK + t * P
                    last = pe.transpose(bank[:, t * P:(t + 1) * P], tile[:, at:at + P], ident[:, :])
                last.then_inc(done, 1)

            def times_blocks(bank, tile_t, c, blocks, done, t0=0, t1=TILES):
                for t in range(t0, t1):
                    at = c * BANK + t * P
                    last = pe.matmul(bank[:, t * P:(t + 1) * P], tile_t[:, at:at + P], blocks[:, :],
                                     start=True, stop=True)
                last.then_inc(done, 1)

            pe.wait_ge(x_loaded, 16)
            pe.wait_ge(ident_ready, 3)
            for c in range(CHUNKS):
                turn_chunk(acc[:, c, :], xrow, c, x_turned)
            pe.wait_ge(small_loaded, 3 * 16)
            pe.wait_ge(zeros_ready, 1)
            for c in range(CHUNKS):
                pe.wait_ge(xt_copied, c + 1)
                times_blocks(acc[:, c, :], xt, c, w_ui if c < USER_CHUNKS else w_ii, xw_ready)
            for c in range(CHUNKS):
                pe.wait_ge(xw_scaled, c + 1)
                last = pe.matmul(acc[:, c, :], zeros[:, 0:P], zeros[:, :], start=True, stop=False,
                                 skip_group_check=True)
            pe.wait_ge(e_ready, CHUNKS)

            def turn_group(k, u, r):
                c, t = plan_of(k).turned[r]
                if c not in {before for before, _ in plan_of(k).turned[:r]}:
                    pe.wait_ge(landed[u][c], k * 16 + 16)
                for h in range(HALVES):
                    for f in range(HALVES):
                        last = pe.transpose(turn_bank(r, h)[:, f * P:(f + 1) * P],
                                            piece(u, c, f, h)[:, t * P:(t + 1) * P], ident[:, :])
                last.then_inc(dve_turned if r % 2 else act_turned, 1)

            def first_product(group, rows_of, start=False, stop=False):
                for h in range(HALVES):
                    last = pe.matmul(yt_ps[h * D:(h + 1) * D, :], e_tile(*group, h), rows_of(h),
                                     start=start, stop=stop)
                return last

            def first_turned(k, u, r):
                plan = plan_of(k)
                pe.wait_ge(dve_copied if r % 2 else act_copied,
                           count_at(k, u, segments_of, r // 2 + 1))
                return first_product(plan.turned[r], lambda h: turned(r, h), stop=(r == len(plan.turned) - 1))

            def first_loaded(k, u, i):
                plan = plan_of(k)
                if i % 2 == 0:
                    pe.wait_ge(rows_landed[buffer(k, u, i // 2)], rows_landings(k, u, i // 2))
                last = first_product(plan.loaded[i], lambda h: loaded(k, u, i, h), start=(i == 0))
                if i % 2 == 1:
                    last.then_inc(rows_used, 1)
                return last

            def second_product(k, u, part):
                c, f = CHUNK_ORDER[part // HALVES], part % HALVES
                if part == 0:
                    pe.wait_ge(y_copied, k * SLOTS + (u + 1))
                if f == 0:
                    pe.wait_ge(landed[u % SLOTS][c], k * 16 + (16 if u >= 0 else 0))
                u %= SLOTS
                for h in range(HALVES):
                    last = pe.matmul(acc[h * D:(h + 1) * D, c, :], y_sb[:, f * D:(f + 1) * D], piece(u, c, f, h),
                                     start=False, stop=False, skip_group_check=True)
                if f == HALVES - 1:
                    last.then_inc(second_done, 1)

            def sum_y(k, u):
                pe.wait_ge(yt_copied, k * SLOTS + (u + 1))
                for f in range(HALVES):
                    last = pe.matmul(y_ps[:, f * D:(f + 1) * D], yt_sb[:, f * P:(f + 1) * P], stacked[:, :],
                                     start=True, stop=True)
                last.then_inc(y_summed, 1)

            def round_of_pass_1(k):
                plan = plan_of(k)
                for u in range(SLOTS):
                    part = CHUNKS * HALVES if isinstance(k, int) and k == 0 and u == 0 else 0
                    i = 0
                    for segment in range(plan.segments):
                        for r in (2 * segment, 2 * segment + 1):
                            turn_group(k, u, r)
                        for _ in range(plan.second_in[segment]):
                            if part < CHUNKS * HALVES:
                                second_product(k, u - 1, part)
                                part += 1
                        for _ in range(plan.loaded_in[segment]):
                            first_loaded(k, u, i)
                            i += 1
                        for r in (2 * segment, 2 * segment + 1):
                            last = first_turned(k, u, r)
                    last.then_inc(first_done, 1)
                    for part in range(part, CHUNKS * HALVES):
                        second_product(k, u - 1, part)
                    sum_y(k, u)

            round_of_pass_1(0)
            with pe.Fori(1, ROUNDS) as k:
                round_of_pass_1(k)

            def turn_x1(b):
                c, t0, t1 = BATCHES[b]
                pe.wait_ge(normed, 2 * b + 2)
                if b > 0:
                    pe.wait_ge(x1t_copied, b)
                turn_chunk(bank_v, xrow, c, x1_turned, t0, t1)

            def x1_times_b(b):
                c, t0, t1 = BATCHES[b]
                pe.wait_ge(x1t_copied, b + 1)
                if b > 0:
                    pe.wait_ge(xb_copied, b)
                times_blocks(bank_y, e_ht, c, bb, xb_ready, t0, t1)

            for part in range(CHUNKS * HALVES):
                second_product(ROUNDS - 1, SLOTS - 1, part)
                if part == 2:
                    pe.wait_ge(ht_copied, 1)
                    turn_chunk(bank_a, e_ht, CHUNK_ORDER[0], h_turned)
                elif part == 7:
                    turn_x1(0)
                elif part == 8:
                    x1_times_b(0)

            def third_product(u, weights, c, first=False):
                for f in range(HALVES):
                    for h in range(HALVES):
                        last = pe.matmul(acc[h * D:(h + 1) * D, c, :], weights[:, f * D:(f + 1) * D],
                                         piece(u, c, f, h), start=(first and f == 0), stop=False,
                                         skip_group_check=True)
                last.then_inc(third_done, 1)

            def xb_of(c, u):
                at = c * BANK + u * HALVES * D
                return xb[:, at:at + HALVES * D]

            def third_of_panel(k, u, weights, then=None):
                for c in range(CHUNKS):
                    pe.wait_ge(landed[u][c], k * 16 + 16 * (CHUNKS + 1))
                    third_product(u, weights, c)
                    if then:
                        then(c)

            for b in range(len(BATCHES)):
                if b > 0:
                    turn_x1(b)
                    if b < CHUNKS:
                        pe.wait_ge(ht_copied, b + 1)
                        turn_chunk(bank_a, e_ht, CHUNK_ORDER[b], h_turned)
                    x1_times_b(b)
                if b < SLOTS:
                    pe.wait_ge(xb_copied, min(b + 1, 2))
                    weights = xb_of(CHUNK_ORDER[0], b)
                    for to in range(CHUNKS):
                        if b == 0:
                            pe.wait_ge(ht_copied, CHUNK_ORDER.index(to) + 1)
                        third_product(b, weights, to, first=(b == 0))
                else:
                    third_of_panel(0, b - SLOTS, xb_of(0, b - SLOTS))

            def hidden(n):
                c, h = divmod(n, HALVES)
                if n >= 2:
                    pe.wait_ge(tanh_ready, n - 1)
                elif n == 1:
                    pe.wait_ge(xb_copied, len(BATCHES))
                pe.matmul((bank_y if n % 2 else bank_v)[:, :], w1_sb[h * D:(h + 1) * D, :],
                          e_ht[h * D:(h + 1) * D, c * BANK:(c + 1) * BANK],
                          start=True, stop=True).then_inc(hidden_ready, 1)

            def mlp(units):
                hidden(units[0])
                for n in units:
                    c, h = divmod(n, HALVES)
                    if n < units[-1]:
                        hidden(n + 1)
                    pe.wait_ge(tanh_ready, n + 1)
                    pe.matmul(acc[h * D:(h + 1) * D, c, :], w2_sb, tanh_part(n),
                              start=False, stop=False, skip_group_check=True).then_inc(mlp_done, 1)

            for u in range(2, SLOTS):
                mlp(range((u - 2) * CHUNKS, (u - 1) * CHUNKS))
                third_of_panel(0, u, xb_of(0, u))

            def turn_u(c):
                pe.wait_ge(ut_copied, c + 1)
                if c >= 3:
                    pe.wait_ge(z_ready, c - 2)
                turn_chunk((bank_a, bank_v, bank_y)[c % 3], e_ht, c, u_turned)

            def staged(k, u):
                pe.wait_ge(xb_staged, k * SLOTS + (u + 1 - SLOTS))
                return xb_stage[:, u * HALVES * D:(u + 1) * HALVES * D]

            with pe.Fori(1, CHUNKS - 2) as k:
                for u in range(SLOTS):
                    third_of_panel(k, u, staged(k, u))
            k = CHUNKS - 2
            for u in range(SLOTS):
                third_of_panel(k, u, staged(k, u), then=turn_u if u == SLOTS - 1 else None)


def kernel(x, adj, L0_gnn_W_u, L0_gnn_diag_u, L0_gnn_par_u, L0_gnn_W_i, L0_gnn_diag_i, L0_gnn_par_i,
           L0_gnn_ln_gamma, L0_gnn_ln_beta, L1_gnn_t, L1_gnn_B, L1_gnn_W1, L1_gnn_b1, L1_gnn_W2, L1_gnn_b2):
    import numpy as np
    import concourse.bacc as bacc
    from concourse.bass_utils import run_bass_kernel_spmd

    nc = bacc.Bacc("TRN2", target_bir_lowering=False, num_devices=1)
    def blocks(a, b):
        m = np.zeros((P, P), np.float32)
        m[0:D, 0:D], m[D:P, D:P] = a, b
        return m

    def rows_of(panels, plan):
        pairs = by_pair[panels][:, [c * 2 + t // 2 for c, t in plan.loaded_pairs]]
        return pairs.reshape(-1, 2 * GROUP)

    w1 = np.asarray(L1_gnn_W1)
    by_pair = (np.asarray(adj).reshape(HALVES, CHUNKS, 2, 2, P, HALVES, PANELS, P)
               .transpose(6, 1, 2, 4, 3, 0, 5, 7).reshape(PANELS, CHUNKS * 2, P, 2 * GROUP))
    a6 = np.asarray(adj).reshape(HALVES, CHUNKS, BANK, HALVES, CHUNKS, TILES, P)
    laid = {
        "adj": a6.transpose(4, 5, 1, 6, 3, 0, 2).reshape(PANELS * CHUNKS * P, PIECE),
        "adj_rows": np.concatenate([rows_of(slice(0, SLOTS), FIRST), rows_of(slice(SLOTS, PANELS), LATER)]),
        "x": np.asarray(x).reshape(HALVES, CHUNKS, TILES, P, D).transpose(3, 1, 2, 0, 4).reshape(P, CHUNKS * BANK),
        "matrices": np.concatenate([blocks(L0_gnn_W_u, L0_gnn_W_i), blocks(L0_gnn_W_i, L0_gnn_W_i)], axis=1),
        "columns": np.concatenate([
            blocks(np.asarray(L1_gnn_B).T, np.asarray(L1_gnn_B).T), np.tile(w1[0:D], (HALVES, 1)), L1_gnn_W2,
            np.concatenate([L0_gnn_diag_u, L0_gnn_diag_i]).reshape(HALVES, CHUNKS, TILES, P)
            .transpose(3, 1, 2, 0).reshape(P, GROUPS * HALVES),
            w1[D].reshape(P, 1), np.asarray(L1_gnn_b1).reshape(P, 1),
            np.tile(np.asarray(L1_gnn_b2).reshape(D, 1), (HALVES, 1))], axis=1),
        "lines": np.concatenate([L0_gnn_ln_gamma, L0_gnn_ln_beta, L0_gnn_par_u, L0_gnn_par_i, L1_gnn_t]),
    }
    arrays, args = {}, {}
    for name, a in laid.items():
        a = np.ascontiguousarray(a)
        arrays["in_" + name] = a
        args[name] = nc.dram_tensor("in_" + name, a.shape, mybir.dt.from_np(a.dtype), kind="ExternalInput").ap()
    args["out"] = nc.dram_tensor("out_rows", (P, CHUNKS * BANK), F32, kind="ExternalOutput").ap()
    gnn_kernel(nc, **args)
    r = run_bass_kernel_spmd(nc, [arrays], core_ids=[0])
    got = r.results[0]["out_rows"].reshape(P, CHUNKS, TILES, HALVES, D).transpose(3, 1, 2, 0, 4)
    return np.ascontiguousarray(got.reshape(N, D))
```
